# Optimizing a Trainium2 kernel written in Bass

```python
import numpy as np
import jax
import jax.numpy as jnp

def _softmax(x, axis=-1):
    return jax.nn.softmax(x, axis=axis)

def _gelu(x):
    return jax.nn.gelu(x, approximate=True)

def _silu(x):
    return jax.nn.silu(x)

def _sigmoid(x):
    return jax.nn.sigmoid(x)

def _layernorm(x, axis=-1, eps=1e-05):
    m = jnp.mean(x, axis=axis, keepdims=True)
    v = jnp.var(x, axis=axis, keepdims=True)
    return (x - m) / jnp.sqrt(v + eps)

def _scatter_add(tgt, idx, src, axis=0):
    return tgt.at[idx].add(src)

def _segment_sum(src, seg, n):
    return jax.ops.segment_sum(src, seg, n)
kernel_name = 'mk_gnn_preln_d2_gnn_r8_3f8e70'

def setup_inputs(seed: int=0):
    np.random.seed(seed)
    _w = jnp.asarray

    def _rec_inputs():
        import jax
        import jax.numpy as jnp
        _gk = jax.random.key(seed)
        x = -0.000202 + 1 * jax.random.normal(jax.random.fold_in(_gk, 1), (12500, 64), jnp.float32)
        _s = jax.random.randint(jax.random.fold_in(_gk, 2), (100000,), 0, 12500, jnp.int32)
        _d = jax.random.randint(jax.random.fold_in(_gk, 3), (100000,), 0, 12500, jnp.int32)
        _loop = jnp.arange(12500, dtype=jnp.int32)
        src = jnp.concatenate([_s, _d, _loop])
        dst = jnp.concatenate([_d, _s, _loop])
        _o = jnp.argsort(dst, stable=True)
        src = src[_o]
        dst = dst[_o]
        edge_attr_64 = -9.77346e-05 + 0.999888 * jax.random.normal(jax.random.fold_in(_gk, 11), (212500, 64), jnp.float32)
        return (x, src, dst, edge_attr_64)
    x, src, dst, edge_attr_64 = _rec_inputs()

    def _L0_gnn_setup():
        import jax, jax.numpy as jnp
        import numpy as np
        N_NODES = 12500
        N_EDGES = 200000
        D = 64
        N_LAYERS = 3

        def _sage_conv(x, src, dst, Wl, Wr, b, n_nodes):
            msgs = x[src]
            summed = jax.ops.segment_sum(msgs, dst, num_segments=n_nodes)
            cnt = jax.ops.segment_sum(jnp.ones(src.shape[0], x.dtype), dst, num_segments=n_nodes)
            agg = summed / jnp.maximum(cnt, 1.0)[:, None]
            return agg @ Wl + x @ Wr + b
        key = jax.random.key(seed)
        k1, k2, k3, k4 = jax.random.split(key, 4)
        x = jax.random.normal(k1, (N_NODES, D), dtype=jnp.float32)
        edge_index = jax.random.randint(k2, (2, N_EDGES), 0, N_NODES, dtype=jnp.int64)
        scale = 1.0 / np.sqrt(D)
        Wl = jax.random.normal(k3, (N_LAYERS, D, D), dtype=jnp.float32) * scale
        Wr = jax.random.normal(k4, (N_LAYERS, D, D), dtype=jnp.float32) * scale
        b = jnp.zeros((N_LAYERS, D), dtype=jnp.float32)
        return {'x': x, 'edge_index': edge_index, 'Wl': Wl, 'Wr': Wr, 'b': b}
    _L0_gnn_all = _L0_gnn_setup()
    _L0_gnn_in = {k: v for k, v in _L0_gnn_all.items() if k in ('Wl', 'Wr', 'b')}
    del _L0_gnn_all

    def _L1_gnn_setup():
        import jax, jax.numpy as jnp
        import numpy as np
        N_NODES = 6250
        N_EDGES = 100000
        H_DIM = 64

        def scatter_mean(e, receiver, num_segments):
            sums = jax.ops.segment_sum(e, receiver, num_segments=num_segments)
            counts = jax.ops.segment_sum(jnp.ones((e.shape[0],), e.dtype), receiver, num_segments=num_segments)
            return sums / jnp.maximum(counts, 1.0)[:, None]
        key = jax.random.key(seed)
        ks = jax.random.split(key, 10)
        h = H_DIM
        v = jax.random.normal(ks[0], (N_NODES, h), dtype=jnp.float32)
        e = jax.random.normal(ks[1], (N_EDGES, h), dtype=jnp.float32)
        edge_index = jax.random.randint(ks[2], (2, N_EDGES), 0, N_NODES, dtype=jnp.int64)

        def glorot(k, shape):
            fan_in, fan_out = shape
            lim = np.sqrt(6.0 / (fan_in + fan_out)).astype(np.float32)
            return jax.random.uniform(k, shape, jnp.float32, -lim, lim)
        W0 = glorot(ks[3], (2 * h, h))
        b0 = jnp.zeros((h,), jnp.float32)
        W1 = glorot(ks[4], (h, h))
        b1 = jnp.zeros((h,), jnp.float32)
        W2 = glorot(ks[5], (h, h))
        b2 = jnp.zeros((h,), jnp.float32)
        return {'v': v, 'edge_index': edge_index, 'e': e, 'W0': W0, 'b0': b0, 'W1': W1, 'b1': b1, 'W2': W2, 'b2': b2}
    _L1_gnn_all = _L1_gnn_setup()
    _L1_gnn_in = {k: v for k, v in _L1_gnn_all.items() if k in ('W0', 'b0', 'W1', 'b1', 'W2', 'b2')}
    del _L1_gnn_all
    return {'x': x, 'src': src, 'dst': dst, 'edge_attr_64': edge_attr_64, 'L0_gnn_Wl': _L0_gnn_in['Wl'], 'L0_gnn_Wr': _L0_gnn_in['Wr'], 'L0_gnn_b': _L0_gnn_in['b'], 'L1_gnn_W0': _L1_gnn_in['W0'], 'L1_gnn_b0': _L1_gnn_in['b0'], 'L1_gnn_W1': _L1_gnn_in['W1'], 'L1_gnn_b1': _L1_gnn_in['b1'], 'L1_gnn_W2': _L1_gnn_in['W2'], 'L1_gnn_b2': _L1_gnn_in['b2']}

def reference(x, src, dst, edge_attr_64, L0_gnn_Wl, L0_gnn_Wr, L0_gnn_b, L1_gnn_W0, L1_gnn_b0, L1_gnn_W1, L1_gnn_b1, L1_gnn_W2, L1_gnn_b2):
    import jax
    import jax.numpy as jnp

    def _L0_gnn_ref(x, edge_index, Wl, Wr, b):
        import jax, jax.numpy as jnp
        import numpy as np
        N_NODES = 12500
        N_EDGES = 200000
        D = 64
        N_LAYERS = 3

        def _sage_conv(x, src, dst, Wl, Wr, b, n_nodes):
            msgs = x[src]
            summed = jax.ops.segment_sum(msgs, dst, num_segments=n_nodes)
            cnt = jax.ops.segment_sum(jnp.ones(src.shape[0], x.dtype), dst, num_segments=n_nodes)
            agg = summed / jnp.maximum(cnt, 1.0)[:, None]
            return agg @ Wl + x @ Wr + b
        src, dst = (edge_index[0], edge_index[1])
        n = x.shape[0]
        h = x
        for i in range(N_LAYERS - 1):
            h = _sage_conv(h, src, dst, Wl[i], Wr[i], b[i], n)
            h = jax.nn.relu(h)
        h = _sage_conv(h, src, dst, Wl[-1], Wr[-1], b[-1], n)
        return h

    def _L1_gnn_ref(v, edge_index, e, W0, b0, W1, b1, W2, b2):
        import jax, jax.numpy as jnp
        import numpy as np
        N_NODES = 6250
        N_EDGES = 100000
        H_DIM = 64

        def scatter_mean(e, receiver, num_segments):
            sums = jax.ops.segment_sum(e, receiver, num_segments=num_segments)
            counts = jax.ops.segment_sum(jnp.ones((e.shape[0],), e.dtype), receiver, num_segments=num_segments)
            return sums / jnp.maximum(counts, 1.0)[:, None]
        receiver = edge_index[1]
        agg = scatter_mean(e, receiver, v.shape[0])
        x = jnp.concatenate([agg, v], axis=-1)
        x = jax.nn.relu(x @ W0 + b0)
        x = jax.nn.relu(x @ W1 + b1)
        x = x @ W2 + b2
        return x
    edge_index = jnp.stack([src, dst])
    h = jnp.maximum(_layernorm(x, axis=-1), 0.0)
    x = x + _L0_gnn_ref(h, edge_index, L0_gnn_Wl, L0_gnn_Wr, L0_gnn_b)
    h = jnp.maximum(_layernorm(x, axis=-1), 0.0)
    x = x + _L1_gnn_ref(h, edge_index, edge_attr_64, L1_gnn_W0, L1_gnn_b0, L1_gnn_W1, L1_gnn_b1, L1_gnn_W2, L1_gnn_b2)
    return x

_drawn_inputs = setup_inputs


def setup_inputs(seed=0):
    import zlib

    import numpy as np

    out = dict(_drawn_inputs(seed))
    spreads = {'L0_gnn_b': (0.0, 0.1),
     'L1_gnn_b0': (0.0, 0.1),
     'L1_gnn_b1': (0.0, 0.1),
     'L1_gnn_b2': (0.0, 0.1)}
    factors = {}
    for name, (base, spread) in spreads.items():
        noise = np.random.default_rng([zlib.crc32(name.encode()), seed]).standard_normal(out[name].shape)
        drawn = base * np.exp(spread * noise) if base else spread * noise
        out[name] = jnp.asarray(drawn.astype(out[name].dtype))
    for name, factor in factors.items():
        out[name] = (out[name] * factor).astype(out[name].dtype)
    return out
```

```python
from contextlib import ExitStack

import concourse.bass as bass
from concourse import mybir

F32 = mybir.dt.float32
I32 = mybir.dt.int32
ALU = mybir.AluOpType
ACT = mybir.ActivationFunctionType
AX = mybir.AxisListType

N = 12500
E = 212500
D = 64
LAYERS = 3
EPS = 1e-5
GP = 125
GT = N // GP
GE = E // GP


def general_path(nc, x, src, dst, attr, Wl, Wr, b, W0, b0, W1, b1, W2, b2, out):
    with ExitStack() as ctx:
        def sb(name, shape, dt=F32):
            return ctx.enter_context(nc.sbuf_tensor("g_" + name, shape, dt))

        def pb(name, shape, dt=F32):
            return ctx.enter_context(nc.psum_tensor("g_" + name, shape, dt))

        def sem(name):
            return ctx.enter_context(nc.semaphore("g_" + name))

        table = nc.dram_tensor("g_table", (N, D), F32).ap()
        sums = [nc.dram_tensor(f"g_sums{i}", (N + GP, D + 1), F32).ap() for i in range(LAYERS + 1)]
        by_part = "(p t) d -> p t d"

        X = sb("X", [GP, GT, D])
        H = sb("H", [GP, GT, D])
        S = sb("S", [GP, GT, D + 1])
        rcnt = sb("rcnt", [GP, GT])
        stat = sb("stat", [GP, 2, GT])
        src_i = sb("src_i", [GP, GE], I32)
        dst_i = sb("dst_i", [GP, GE], I32)
        ident = sb("ident", [GP, GP])
        earlier = sb("earlier", [GP, GP])
        eq = sb("eq", [GP, GP])
        eqe = sb("eqe", [GP, GP])
        dcol = sb("dcol", [GP, 1])
        dup = sb("dup", [GP, 1])
        spare = sb("spare", [GP, 1])
        at_src = sb("at_src", [GP, 1], I32)
        at_dst = sb("at_dst", [GP, 1], I32)
        msg = sb("msg", [GP, D + 1])
        comb = sb("comb", [GP, D + 1])
        cat = sb("cat", [GP, 2 * D])
        catT = sb("catT", [2 * D, GP])
        y0 = sb("y0", [D, GP])
        y1 = sb("y1", [D, GP])
        w = sb("w", [2 * D, LAYERS, D])
        w0 = sb("w0", [2 * D, D])
        w1 = sb("w1", [D, D])
        w2 = sb("w2", [D, D])
        bias = sb("bias", [GP, LAYERS + 1, D])
        bias01 = sb("bias01", [D, 2])
        ps_dst = pb("ps_dst", [GP, GP])
        ps_comb = pb("ps_comb", [GP, D + 1])
        ps_T = pb("ps_T", [2 * D, GP])
        ps_a = pb("ps_a", [GP, D])
        ps_y0 = pb("ps_y0", [D, GP])
        ps_y1 = pb("ps_y1", [D, GP])

        loaded = sem("loaded")
        constants = sem("constants")
        const_step = sem("const_step")

        def layernorm_relu(steps, of, to):
            m, v = stat[:, 0, :], stat[:, 1, :]
            wide = (GP, GT, D)
            steps(nc.vector.tensor_reduce(m, of, AX.X, ALU.add))
            steps(nc.vector.tensor_scalar(m, m, 1.0 / D, None, ALU.mult))
            steps(nc.vector.tensor_tensor(to, of, m.unsqueeze(2).broadcast_to(wide), ALU.subtract))
            steps(nc.vector.tensor_tensor(S[:, :, 0:D], to, to, ALU.mult))
            steps(nc.vector.tensor_reduce(v, S[:, :, 0:D], AX.X, ALU.add))
            steps(nc.vector.tensor_scalar(v, v, 1.0 / D, EPS, ALU.mult, ALU.add))

        with ExitStack() as part:
            varied = part.enter_context(nc.semaphore("g_varied"))
            rooted = part.enter_context(nc.semaphore("g_rooted"))
            dve_step = part.enter_context(nc.semaphore("g_dve_step0"))
            zeroed = part.enter_context(nc.semaphore("g_zeroed"))
            normed = part.enter_context(nc.semaphore("g_normed"))
            stored = part.enter_context(nc.semaphore("g_stored0"))
            block = part.enter_context(nc.Block())

            @block.sync
            def _(sp):
                sp.dma_start(X[:, :, :], x.rearrange(by_part, p=GP)).then_inc(loaded, 16)
                sp.dma_start(src_i[:, :], src.rearrange("(p j) -> p j", p=GP)).then_inc(loaded, 16)
                sp.dma_start(dst_i[:, :], dst.rearrange("(p j) -> p j", p=GP)).then_inc(loaded, 16)
                sp.dma_start(w[0:D, :, :], Wl.rearrange("l i o -> i l o")).then_inc(loaded, 16)
                sp.dma_start(w[D:2 * D, :, :], Wr.rearrange("l i o -> i l o")).then_inc(loaded, 16)
                sp.dma_start(w0[:, :], W0).then_inc(loaded, 16)
                sp.dma_start(w1[:, :], W1).then_inc(loaded, 16)
                sp.dma_start(w2[:, :], W2).then_inc(loaded, 16)
                for i in range(LAYERS):
                    sp.dma_start(bias[:, i, :], b[i:i + 1, :].broadcast_to((GP, D))).then_inc(loaded, 16)
                sp.dma_start(bias[:, LAYERS, :], b2.unsqueeze(0).broadcast_to((GP, D))).then_inc(loaded, 16)
                sp.dma_start(bias01[:, 0:1], b0.unsqueeze(1)).then_inc(loaded, 16)
                sp.dma_start(bias01[:, 1:2], b1.unsqueeze(1)).then_inc(loaded, 16)
                sp.wait_ge(zeroed, 1)
                for i in range(LAYERS + 1):
                    sp.dma_start(sums[i][0:N, :].rearrange(by_part, p=GP), S[:, :, :]).then_inc(stored, 16)
                    sp.dma_start(sums[i][N:N + GP, :], S[:, 0, :]).then_inc(stored, 16)
                sp.wait_ge(normed, 1)
                sp.dma_start(table.rearrange(by_part, p=GP), H[:, :, :]).then_inc(stored, 16)
                sp.wait_ge(stored, 16 * (2 * LAYERS + 3))
                sp.wait_ge(loaded, 16 * 14)

            @block.gpsimd
            def _(pool):
                nc.gpsimd.memset(ident[:, :], 0.0).then_inc(const_step, 1)
                nc.gpsimd.memset(earlier[:, :], 1.0).then_inc(const_step, 1)
                pool.wait_ge(const_step, 2)
                nc.gpsimd.affine_select(out=ident[:, :], in_=ident[:, :], compare_op=ALU.not_equal, fill=1.0,
                                        base=0, pattern=[[-1, GP]], channel_multiplier=1).then_inc(constants, 1)
                nc.gpsimd.affine_select(out=earlier[:, :], in_=earlier[:, :], compare_op=ALU.is_gt, fill=0.0,
                                        base=0, pattern=[[-1, GP]], channel_multiplier=1).then_inc(constants, 1)
                nc.gpsimd.memset(msg[:, :], 1.0).then_inc(constants, 1)
                nc.gpsimd.iota(spare[:, :], pattern=[[0, 1]], base=N, channel_multiplier=1,
                               allow_small_or_imprecise_dtypes=True).then_inc(constants, 1)

            @block.scalar
            def _(act):
                act.wait_ge(varied, 1)
                nc.scalar.activation(stat[:, 1, :], stat[:, 1, :], ACT.Sqrt).then_inc(rooted, 1)

            @block.vector
            def _(dve):
                count = [0]

                def steps(ins):
                    count[0] += 1
                    ins.then_inc(dve_step, 1)
                    dve.wait_ge(dve_step, count[0])

                nc.vector.memset(S[:, :, :], 0.0).then_inc(zeroed, 1)
                dve.wait_ge(loaded, 16 * 14)
                dve.wait_ge(stored, 16 * (2 * LAYERS + 2))
                layernorm_relu(steps, X[:, :, :], H[:, :, :])
                nc.vector.tensor_copy(stat[:, 0, :], stat[:, 0, :]).then_inc(varied, 1)
                dve.wait_ge(rooted, 1)
                steps(nc.vector.reciprocal(stat[:, 1, :], stat[:, 1, :]))
                steps(nc.vector.tensor_tensor(H[:, :, :], H[:, :, :],
                                              stat[:, 1, :].unsqueeze(2).broadcast_to((GP, GT, D)), ALU.mult))
                nc.vector.tensor_scalar(H[:, :, :], H[:, :, :], 0.0, None, ALU.max).then_inc(normed, 1)

        def edge_block(i):
            with ExitStack() as part:
                def s(name):
                    return part.enter_context(nc.semaphore(f"g_{name}{i}"))

                turns, indexed, transposed, equal, summed, ready = s("turns"), s("indexed"), s("transposed"), s("equal"), s("summed"), s("ready")
                gathered, scattered, dve_step = s("gathered"), s("scattered"), s("dve_step")
                block = part.enter_context(nc.Block())

                @block.gpsimd
                def _(pool):
                    with pool.Fori(0, GE) as j:
                        pool.wait_ge(indexed, j + 1)
                        pool.sem_inc(turns, 1)
                        if i < LAYERS:
                            nc.gpsimd.indirect_dma_start(
                                out=msg[:, 0:D], out_offset=None, in_=table[:, :],
                                in_offset=bass.IndirectOffsetOnAxis(ap=at_src[:, 0:1], axis=0)).then_inc(gathered, 16)
                        else:
                            pool.dma_start(msg[:, 0:D],
                                           attr.rearrange("(p j) d -> p j d", p=GP)[:, bass.ds(j, 1), :]
                                           .rearrange("p j d -> p (j d)")).then_inc(gathered, 16)
                        pool.wait_ge(ready, j + 1)
                        pool.sem_inc(turns, 1)
                        nc.gpsimd.indirect_dma_start(
                            out=sums[i][:, :], out_offset=bass.IndirectOffsetOnAxis(ap=at_dst[:, 0:1], axis=0),
                            in_=comb[:, :], in_offset=None,
                            compute_op=ALU.add).then_inc(scattered, 16)
                        pool.wait_ge(scattered, 16 * j + 16)

                @block.tensor
                def _(pe):
                    with pe.Fori(0, GE) as j:
                        pe.wait_ge(indexed, j + 1)
                        nc.tensor.transpose(ps_dst[:, :], dcol[:, 0:1].broadcast_to((GP, GP)), ident[:, :]).then_inc(transposed, 1)
                        pe.wait_ge(equal, j + 1)
                        pe.wait_ge(gathered, 16 * j + 16)
                        nc.tensor.matmul(ps_comb[:, :], eq[:, :], msg[:, :], start=True, stop=True).then_inc(summed, 1)

                @block.vector
                def _(dve):
                    with dve.Fori(0, GE) as j:
                        def step(ins, k):
                            ins.then_inc(dve_step, 1)
                            dve.wait_ge(dve_step, 6 * j + k)

                        step(nc.vector.tensor_copy(at_src[:, :], src_i[:, bass.ds(j, 1)]), 1)
                        nc.vector.tensor_copy(dcol[:, :], dst_i[:, bass.ds(j, 1)]).then_inc(indexed, 1)
                        dve.wait_ge(transposed, j + 1)
                        step(nc.vector.tensor_scalar(eq[:, :], ps_dst[:, :], dcol[:, 0:1], None, ALU.is_equal), 2)
                        step(nc.vector.tensor_tensor(eqe[:, :], eq[:, :], earlier[:, :], ALU.mult), 3)
                        step(nc.vector.tensor_reduce(dup[:, :], eqe[:, :], AX.X, ALU.max), 4)
                        step(nc.vector.tensor_scalar(dup[:, :], spare[:, :], dcol[:, 0:1], dup[:, 0:1],
                                                     ALU.subtract, ALU.mult), 5)
                        nc.vector.tensor_tensor(at_dst[:, :], dup[:, :], dcol[:, :], ALU.add).then_inc(equal, 1)
                        dve.wait_ge(summed, j + 1)
                        step(nc.vector.tensor_copy(comb[:, :], ps_comb[:, :]), 6)
                        nc.vector.tensor_copy(dup[:, :], dup[:, :]).then_inc(ready, 1)
                        dve.wait_ge(scattered, 16 * j + 16)

        def node_block(i):
            last = i == LAYERS
            with ExitStack() as part:
                def s(name):
                    return part.enter_context(nc.semaphore(f"g_{name}n{i}"))

                landed, joined, turned, turned_sb, mixed = s("landed"), s("joined"), s("turned"), s("turned_sb"), s("mixed")
                y0_ps, y0_sb, y1_ps, y1_sb, done, stored, dve_step = (
                    s("y0_ps"), s("y0_sb"), s("y1_ps"), s("y1_sb"), s("done"), s("stored"), s("dve_step"))
                varied, rooted = s("varied"), s("rooted")
                block = part.enter_context(nc.Block())
                to_dram = out if last else table

                @block.sync
                def _(sp):
                    sp.dma_start(S[:, :, :], sums[i][0:N, :].rearrange(by_part, p=GP)).then_inc(landed, 16)
                    if i == LAYERS - 1:
                        return
                    sp.wait_ge(done, 1)
                    sp.dma_start(to_dram.rearrange(by_part, p=GP), (X if last else H)[:, :, :]).then_inc(stored, 16)
                    sp.wait_ge(stored, 16)

                @block.tensor
                def _(pe):
                    with pe.Fori(0, GT) as t:
                        pe.wait_ge(joined, t + 1)
                        nc.tensor.transpose(ps_T[:, :], cat[:, :], ident[:, :]).then_inc(turned, 1)
                        pe.wait_ge(turned_sb, t + 1)
                        if not last:
                            nc.tensor.matmul(ps_a[:, :], catT[:, :], w[:, i, :], start=True, stop=True).then_inc(mixed, 1)
                        else:
                            nc.tensor.matmul(ps_y0[:, :], w0[:, :], catT[:, :], start=True, stop=True).then_inc(y0_ps, 1)
                            pe.wait_ge(constants, 4)
                            pe.wait_ge(y0_sb, t + 1)
                            nc.tensor.matmul(ps_y1[:, :], w1[:, :], y0[:, :], start=True, stop=True).then_inc(y1_ps, 1)
                            pe.wait_ge(constants, 4)
                            pe.wait_ge(y1_sb, t + 1)
                            nc.tensor.matmul(ps_a[:, :], y1[:, :], w2[:, :], start=True, stop=True).then_inc(mixed, 1)

                @block.scalar
                def _(act):
                    if last:
                        with act.Fori(0, GT) as t:
                            act.wait_ge(y0_ps, t + 1)
                            nc.scalar.activation(y0[:, :], ps_y0[:, :], ACT.Relu, bias=bias01[:, 0:1]).then_inc(y0_sb, 1)
                            act.wait_ge(y1_ps, t + 1)
                            nc.scalar.activation(y1[:, :], ps_y1[:, :], ACT.Relu, bias=bias01[:, 1:2]).then_inc(y1_sb, 1)
                    if i == LAYERS - 1:
                        act.wait_ge(varied, 1)
                        nc.scalar.activation(stat[:, 1, :], stat[:, 1, :], ACT.Sqrt).then_inc(rooted, 1)

                @block.vector
                def _(dve):
                    dve.wait_ge(landed, 16)
                    nc.vector.tensor_scalar(rcnt[:, :], S[:, :, D], 1.0, None, ALU.max).then_inc(dve_step, 1)
                    dve.wait_ge(dve_step, 1)
                    nc.vector.reciprocal(rcnt[:, :], rcnt[:, :]).then_inc(dve_step, 1)
                    dve.wait_ge(dve_step, 2)
                    with dve.Fori(0, GT) as t:
                        def step(ins, k):
                            ins.then_inc(dve_step, 1)
                            dve.wait_ge(dve_step, 3 * t + 2 + k)

                        def row(a):
                            return a[:, bass.ds(t, 1), 0:D].rearrange("p t d -> p (t d)")

                        step(nc.vector.tensor_scalar(cat[:, 0:D], row(S), rcnt[:, bass.ds(t, 1)], None, ALU.mult), 1)
                        nc.vector.tensor_copy(cat[:, D:2 * D], row(H)).then_inc(joined, 1)
                        dve.wait_ge(turned, t + 1)
                        nc.vector.tensor_copy(catT[:, :], ps_T[:, :]).then_inc(turned_sb, 1)
                        dve.wait_ge(mixed, t + 1)
                        if i < LAYERS - 1:
                            step(nc.vector.tensor_tensor(row(H), ps_a[:, :], bias[:, i, :], ALU.add), 2)
                            step(nc.vector.tensor_scalar(row(H), row(H), 0.0, None, ALU.max), 3)
                        else:
                            step(nc.vector.tensor_tensor(row(H), ps_a[:, :], bias[:, i, :], ALU.add), 2)
                            step(nc.vector.tensor_tensor(row(X), row(H), row(X), ALU.add), 3)
                    count = [3 * GT + 2]

                    def steps(ins):
                        count[0] += 1
                        ins.then_inc(dve_step, 1)
                        dve.wait_ge(dve_step, count[0])

                    if i == LAYERS - 1:
                        layernorm_relu(steps, X[:, :, :], H[:, :, :])
                        nc.vector.tensor_copy(stat[:, 0, :], stat[:, 0, :]).then_inc(varied, 1)
                        dve.wait_ge(rooted, 1)
                        steps(nc.vector.reciprocal(stat[:, 1, :], stat[:, 1, :]))
                        steps(nc.vector.tensor_tensor(H[:, :, :], H[:, :, :],
                                                      stat[:, 1, :].unsqueeze(2).broadcast_to((GP, GT, D)), ALU.mult))
                        steps(nc.vector.tensor_scalar(H[:, :, :], H[:, :, :], 0.0, None, ALU.max))
                    nc.vector.tensor_copy(rcnt[:, :], rcnt[:, :]).then_inc(done, 1)

        for i in range(LAYERS + 1):
            edge_block(i)
            node_block(i)


_INS = ['x', 'src', 'dst', 'edge_attr_64', 'L0_gnn_Wl', 'L0_gnn_Wr', 'L0_gnn_b', 'L1_gnn_W0', 'L1_gnn_b0',
        'L1_gnn_W1', 'L1_gnn_b1', 'L1_gnn_W2', 'L1_gnn_b2']


def kernel(**inputs):
    import numpy as _np
    import concourse.bacc as _bacc
    from concourse import mybir as _mybir
    from concourse.bass_utils import run_bass_kernel_spmd as _run

    nc = _bacc.Bacc("TRN2", target_bir_lowering=False, num_devices=1)
    arrays, args = {}, []
    for name in _INS:
        a = _np.ascontiguousarray(inputs[name])
        arrays[f"in_{name}"] = a
        args.append(nc.dram_tensor(f"in_{name}", a.shape, _mybir.dt.from_np(a.dtype), kind="ExternalInput").ap())
    out = nc.dram_tensor("out_0", (N, D), _mybir.dt.float32, kind="ExternalOutput").ap()
    general_path(nc, *args, out)
    r = _run(nc, [arrays], core_ids=[0])
    return r.results[0]["out_0"]
```

```python
from contextlib import ExitStack

import concourse.bass as bass
from concourse import mybir

F32 = mybir.dt.float32
F16 = mybir.dt.float16
F8 = mybir.dt.float8e4
I32 = mybir.dt.int32
U8 = mybir.dt.uint8
ALU = mybir.AluOpType
ACT = mybir.ActivationFunctionType
AX = mybir.AxisListType

N = 12500
E = 212500
D = 64
LAYERS = 3
EPS = 1e-5
GP = 125
GT = N // GP
GE = E // GP

P = 128
LO = 125
HI = N // LO
G = 5
BLOCK = 500
NB = N // BLOCK
GROUPS = BLOCK // G
SUBS = BLOCK // LO
PAIR = 2
UNITS = GROUPS // PAIR
OH_SLOTS = 5
PS_SLOTS = 2
ROW = 425
ROWS = E // ROW
MAX_COUNT = 15.5
LOW_SCALE = 2048.0
MAX_H = 60000.0
CHUNKS = 5
CHUNK = HI // CHUNKS
SC = 4
SR = 17
NS = NB * SC
SPAN = 152
DMA_P = 112
assert LO * SR * NS == E and GROUPS * G * NB == N and ROW * ROWS == E


def dense_path(nc, x, src, dst, attr, Wl, Wr, b, W0, b0, W1, b1, W2, b2, out, verdict):
    with ExitStack() as ctx:
        def sb(name, shape, dt=F32, stack=ctx):
            return stack.enter_context(nc.sbuf_tensor(name, shape, dt))

        def pb(name, shape, dt=F32, stack=ctx):
            return stack.enter_context(nc.psum_tensor(name, shape, dt))

        def sem(name, stack=ctx):
            return stack.enter_context(nc.semaphore(name))

        matrix = nc.dram_tensor("matrix", (NB, P, HI * BLOCK), U8).ap()
        h_T = [nc.dram_tensor(f"h_T{i}", (D, N), F32).ap() for i in range(LAYERS)]
        rcnt_d = nc.dram_tensor("rcnt_d", (1, N), F32).ap()

        H = [sb(f"H{i}", [LO, HI, 2 * D], F16) for i in range(2)]
        low = sb("low", [P, GROUPS * NB], F16)
        col = sb("col", [P, GROUPS * NB], F16)
        rel = sb("rel", [LO, NS * SR], F16)
        base_i = sb("base_i", [1, NS], I32)
        ident = sb("ident", [P, P])
        wl = sb("wl", [P, LAYERS, D])
        wr = sb("wr", [D, LAYERS, D])
        w0a = sb("w0a", [D, D])
        w0v = sb("w0v", [D, D])
        w1 = sb("w1", [D, D])
        w2 = sb("w2", [D, D])
        biases = sb("biases", [D, LAYERS + 2])
        b2_bc = sb("b2_bc", [LO, SUBS, D])
        flags = sb("flags", [P, 4])

        ps_build = [pb(f"ps_build{i}", [P, PAIR, 512]) for i in range(PS_SLOTS)]
        ps_S = [pb(f"ps_S{i}", [P, 512]) for i in range(2)]
        ps_mix = pb("ps_mix", [P, 512])
        ps_turn = pb("ps_turn", [P, 512])

        constants = sem("constants")
        sp_turns, act_turns, pe_turns, pool_turns = sem("sp_turns"), sem("act_turns"), sem("pe_turns"), sem("pool_turns")

        def by_tile(a):
            return a.rearrange("(h p) d -> p h d", p=LO)

        with ExitStack() as part:
            def psb(name, shape, dt=F32):
                return sb("p_" + name, shape, dt, part)

            X = psb("X", [LO, HI, D])
            Y = psb("Y", [LO, HI, D])
            stat = psb("stat", [LO, 3, HI])
            heads_i = psb("heads_i", [1, ROWS], I32)
            heads_f = psb("heads_f", [1, ROWS])
            heads = psb("heads", [GROUPS, ROWS])
            ones = psb("ones", [1, P])
            limit_i = psb("limit_i", [GROUPS, NB], I32)
            limit = psb("limit", [GROUPS, NB])
            row_f = psb("row_f", [GROUPS, NB])
            row_i = psb("row_i", [GROUPS, NB], I32)
            begin_f = psb("begin_f", [GROUPS, NB])
            begin_i = psb("begin_i", [GROUPS, NB], I32)
            rows = psb("rows", [GROUPS, 4, ROW], I32)
            below = psb("below", [GROUPS, 512])
            ws = psb("ws", [GROUPS, NB, P], I32)
            wd = psb("wd", [GROUPS, NB, P], I32)
            hi_f = psb("hi_f", [GROUPS, NB, P])
            lo_f = ws[:, :, :].bitcast(F32)
            off = wd[:, :, :].bitcast(F32)
            ok = X[0:GROUPS, 0:HI // 2, :].rearrange("p h d -> p (h d)").rearrange("p (t e) -> p t e", t=NB)
            rel_i = psb("rel_i", [LO, NS, SR], I32)
            base_f = psb("base_f", [1, NS])
            Y2 = X[:, :, :].rearrange("p h d -> p (h d)")
            cnt = psb("cnt", [GROUPS, NB, G])
            hT_sb = psb("hT_sb", [D, 2, BLOCK])

            def ps(name):
                return sem("p_" + name, part)

            ld_x, ld_heads, ld_w = ps("ld_x"), ps("ld_heads"), ps("ld_w")
            heads_f_ok, heads_ps, row_ok, begin_ok, c_ok = ps("heads_f_ok"), ps("heads_ps"), ps("row_ok"), ps("begin_ok"), ps("c_ok")
            row_in = [ps(f"row_in{i}") for i in range(4)]
            row_used, win_in, limits_ok = ps("row_used"), ps("win_in"), ps("limits_ok")
            idx_turned, idx_copied, dve_step, act_step = ps("idx_turned"), ps("idx_copied"), ps("dve_step"), ps("act_step")
            varied, rooted, normed, h_turned, h_copied = (
                ps("varied"), ps("rooted"), ps("normed"), ps("h_turned"), ps("h_copied"))
            h_stored = [ps("h_stored0"), ps("h_stored1")]
            squared, centred, cnt_ok, cnt_stored, pool_step, halved = (
                ps("squared"), ps("centred"), ps("cnt_ok"), ps("cnt_stored"), ps("pool_step"), ps("halved"))
            ld_rel, base_f_ok, base_ps = ps("ld_rel"), ps("base_f_ok"), ps("base_ps")
            block = part.enter_context(nc.Block())

            @block.sync
            def _(sp):
                sp.dma_start(heads_i[:, :], dst.rearrange("(o r c) -> o r c", o=1, c=ROW)[:, :, 0],
                             allow_slow_non_contiguous=True).then_inc(ld_heads, 16)
                sp.dma_start(X[:, :, :], by_tile(x)).then_inc(ld_x, 16)
                sp.dma_start(base_i[:, :], dst.rearrange("(o s c) -> o s c", o=1, c=LO * SR)[:, :, 0],
                             allow_slow_non_contiguous=True).then_inc(ld_rel, 16)
                sp.dma_start(rel_i[:, :, :], dst.rearrange("(s p r) -> p s r", p=LO, r=SR)).then_inc(ld_rel, 16)
                sp.dma_start(wl[0:D, :, :], Wl.rearrange("l i o -> i l o")).then_inc(ld_w, 16)
                sp.dma_start(wl[D:P, :, :], Wl.rearrange("l i o -> i l o")).then_inc(ld_w, 16)
                sp.dma_start(wr[:, :, :], Wr.rearrange("l i o -> i l o")).then_inc(ld_w, 16)
                sp.dma_start(w0a[:, :], W0[0:D, :]).then_inc(ld_w, 16)
                sp.dma_start(w0v[:, :], W0[D:2 * D, :]).then_inc(ld_w, 16)
                sp.dma_start(w1[:, :], W1).then_inc(ld_w, 16)
                sp.dma_start(w2[:, :], W2).then_inc(ld_w, 16)
                for i in range(LAYERS):
                    sp.dma_start(biases[:, i:i + 1], b[i, :].unsqueeze(1)).then_inc(ld_w, 16)
                sp.dma_start(biases[:, LAYERS:LAYERS + 1], b0.unsqueeze(1)).then_inc(ld_w, 16)
                sp.dma_start(biases[:, LAYERS + 1:LAYERS + 2], b1.unsqueeze(1)).then_inc(ld_w, 16)
                for k in range(SUBS):
                    sp.dma_start(b2_bc[:, k, :], b2.unsqueeze(0).broadcast_to((LO, D))).then_inc(ld_w, 16)
                for t in range(NB):
                    sp.wait_ge(h_copied, t + 1)
                    sp.dma_start(h_T[0][:, BLOCK * t:BLOCK * (t + 1)], hT_sb[:, t % 2, :]).then_inc(h_stored[t % 2], 16)
                sp.wait_ge(cnt_ok, 1)
                sp.dma_start(rcnt_d.rearrange("o (b g f) -> (o g) b f", g=GROUPS, f=G), cnt[:, :, :]).then_inc(cnt_stored, 16)
                sp.wait_ge(cnt_stored, 16)
                sp.wait_ge(h_stored[0], 16 * ((NB + 1) // 2))
                sp.wait_ge(h_stored[1], 16 * (NB // 2))
                sp.wait_ge(ld_w, 16 * 16)

            @block.gpsimd
            def _(pool):
                nc.gpsimd.memset(ones[:, :], 1.0).then_inc(constants, 1)
                nc.gpsimd.iota(limit_i[:, :], pattern=[[BLOCK, NB]], base=0, channel_multiplier=G).then_inc(limits_ok, 1)
                nc.gpsimd.memset(ident[:, :], 0.0).then_inc(pool_step, 1)
                nc.gpsimd.memset(flags[:, :], 0.0).then_inc(constants, 1)
                pool.wait_ge(pool_step, 1)
                nc.gpsimd.affine_select(out=ident[:, :], in_=ident[:, :], compare_op=ALU.not_equal, fill=1.0,
                                        base=0, pattern=[[-1, P]], channel_multiplier=1).then_inc(constants, 1)
                pool.wait_ge(row_ok, 1)
                for t in range(NB):
                    if t >= 4:
                        pool.wait_ge(row_used, t - 3)
                    nc.gpsimd.indirect_dma_start(
                        out=rows[:, t % 4, :], out_offset=None, in_=dst.rearrange("(r c) -> r c", c=ROW),
                        in_offset=bass.IndirectOffsetOnAxis(ap=row_i[:, t:t + 1], axis=0)).then_inc(row_in[t % 4], 16)
                pool.wait_ge(begin_ok, 1)
                for t in range(NB):
                    for list_, to in ((dst, wd), (src, ws)):
                        nc.gpsimd.indirect_dma_start(
                            out=to[:, t, :], out_offset=None, in_=list_.unsqueeze(1),
                            in_offset=bass.IndirectOffsetOnAxis(ap=begin_i[:, t:t + 1], axis=0)).then_inc(win_in, 16)
                pool.wait_ge(win_in, 16 * 2 * NB)

            @block.tensor
            def _(pe):
                pe.wait_ge(constants, 3)
                pe.wait_ge(heads_f_ok, 1)
                nc.tensor.matmul(ps_S[0][0:GROUPS, 0:ROWS], ones[:, 0:GROUPS], heads_f[:, :], start=True, stop=True).then_inc(heads_ps, 1)
                pe.wait_ge(base_f_ok, 1)
                nc.tensor.matmul(ps_mix[0:LO, 0:NS], ones[:, 0:LO], base_f[:, :], start=True, stop=True).then_inc(base_ps, 1)
                pe.wait_ge(normed, 1)
                for t in range(NB):
                    if t >= 2:
                        pe.wait_ge(h_copied, t - 1)
                    for k in range(SUBS):
                        last = nc.tensor.transpose(ps_build[t % 2][0:D, 0, LO * k:LO * (k + 1)], Y[:, SUBS * t + k, :], ident[0:LO, 0:LO])
                    last.then_inc(h_turned, 1)
                pe.wait_ge(c_ok, 1)
                for t in range(NB):
                    if t >= 2:
                        pe.wait_ge(idx_copied, t - 1)
                    nc.tensor.transpose(ps_S[t % 2][:, 0:GROUPS], lo_f[:, t, :], ident[0:GROUPS, 0:GROUPS])
                    nc.tensor.transpose(ps_S[t % 2][:, 256:256 + GROUPS], hi_f[:, t, :], ident[0:GROUPS, 0:GROUPS]).then_inc(idx_turned, 1)

            @block.scalar
            def _(act):
                act.wait_ge(centred, 1)
                nc.scalar.activation(X[:, :, :], Y[:, :, :], ACT.Square).then_inc(squared, 1)
                act.wait_ge(varied, 1)
                nc.scalar.activation(stat[:, 1, :], stat[:, 1, :], ACT.Sqrt).then_inc(rooted, 1)
                act.wait_ge(normed, 1)
                nc.scalar.activation(H[0][:, :, 0:D], Y[:, :, :], ACT.Copy).then_inc(act_step, 1)
                act.wait_ge(act_step, 1)
                nc.scalar.activation(X[:, :, :], H[0][:, :, 0:D], ACT.Copy, scale=LOW_SCALE).then_inc(halved, 1)
                for t in range(NB):
                    act.wait_ge(h_turned, t + 1)
                    if t >= 2:
                        act.wait_ge(h_stored[t % 2], 16 * (t // 2))
                    nc.scalar.copy(hT_sb[:, t % 2, :], ps_build[t % 2][0:D, 0, 0:BLOCK]).then_inc(h_copied, 1)
                for t in range(NB):
                    act.wait_ge(idx_turned, t + 1)
                    nc.scalar.copy(low[:, GROUPS * t:GROUPS * (t + 1)], ps_S[t % 2][:, 0:GROUPS])
                    nc.scalar.copy(col[:, GROUPS * t:GROUPS * (t + 1)], ps_S[t % 2][:, 256:256 + GROUPS]).then_inc(idx_copied, 1)

            @block.vector
            def _(dve):
                count = [0]

                def step(ins):
                    count[0] += 1
                    ins.then_inc(dve_step, 1)
                    dve.wait_ge(dve_step, count[0])

                dve.wait_ge(constants, 3)
                def norm():
                    m = stat[:, 0, :]
                    step(nc.vector.tensor_reduce(m, X[:, :, :], AX.X, ALU.add))
                    step(nc.vector.tensor_scalar(m, m, 1.0 / D, None, ALU.mult))
                    nc.vector.tensor_tensor(Y[:, :, :], X[:, :, :], m.unsqueeze(2).broadcast_to((LO, HI, D)),
                                            ALU.subtract).then_inc(centred, 1)

                dve.wait_ge(ld_heads, 16)
                nc.vector.tensor_copy(heads_f[:, :], heads_i[:, :]).then_inc(heads_f_ok, 1)
                dve.wait_ge(limits_ok, 1)
                step(nc.vector.tensor_copy(limit[:, :], limit_i[:, :]))
                dve.wait_ge(heads_ps, 1)
                step(nc.vector.tensor_copy(heads[:, :], ps_S[0][0:GROUPS, 0:ROWS]))
                for t in range(NB):
                    step(nc.vector.tensor_scalar(below[:, 0:ROWS], heads[:, :], limit[:, t:t + 1], 0.0, ALU.is_lt, ALU.add,
                                                 accum_out=row_f[:, t:t + 1]))
                step(nc.vector.tensor_scalar(row_f[:, :], row_f[:, :], -1.0, 0.0, ALU.add, ALU.max))
                nc.vector.tensor_copy(row_i[:, :], row_f[:, :]).then_inc(row_ok, 1)
                dve.wait_ge(ld_x, 16)
                norm()
                for t in range(NB):
                    dve.wait_ge(row_in[t % 4], 16 * (t // 4 + 1))
                    step(nc.vector.tensor_copy(below[:, 0:ROW], rows[:, t % 4, :]))
                    step(nc.vector.tensor_scalar(below[:, 0:ROW], below[:, 0:ROW], limit[:, t:t + 1], 0.0, ALU.is_lt, ALU.add,
                                                 accum_out=begin_f[:, t:t + 1]))
                    dve.sem_inc(row_used, 1)
                step(nc.vector.scalar_tensor_tensor(begin_f[:, :], row_f[:, :], float(ROW), begin_f[:, :], ALU.mult, ALU.add))
                step(nc.vector.tensor_scalar(begin_f[:, :], begin_f[:, :], float(E - P), None, ALU.min))
                nc.vector.tensor_copy(begin_i[:, :], begin_f[:, :]).then_inc(begin_ok, 1)
                dve.wait_ge(squared, 1)
                v = stat[:, 1, :]
                step(nc.vector.tensor_reduce(v, X[:, :, :], AX.X, ALU.add))
                nc.vector.tensor_scalar(v, v, 1.0 / D, EPS, ALU.mult, ALU.add).then_inc(varied, 1)
                dve.wait_ge(rooted, 1)
                step(nc.vector.reciprocal(v, v))
                step(nc.vector.tensor_tensor(Y[:, :, :], Y[:, :, :], v.unsqueeze(2).broadcast_to((LO, HI, D)), ALU.mult))
                nc.vector.tensor_scalar(Y[:, :, :], Y[:, :, :], 0.0, None, ALU.max).then_inc(normed, 1)
                dve.wait_ge(halved, 1)
                step(nc.vector.scalar_tensor_tensor(H[0][:, :, D:2 * D], Y[:, :, :], LOW_SCALE, X[:, :, :], ALU.mult, ALU.subtract))
                dve.wait_ge(ld_w, 16 * 16)
                step(nc.vector.tensor_scalar(wl[D:P, :, :], wl[D:P, :, :], 1.0 / LOW_SCALE, None, ALU.mult))
                dve.wait_ge(ld_rel, 32)
                nc.vector.tensor_copy(base_f[:, :], base_i[:, :]).then_inc(base_f_ok, 1)
                rel_f = Y2[:, NS * SR:2 * NS * SR]
                rel3 = rel_f.rearrange("p (s r) -> p s r", r=SR)
                step(nc.vector.tensor_copy(rel3, rel_i[:, :, :]))
                dve.wait_ge(base_ps, 1)
                step(nc.vector.tensor_tensor(rel3, rel3, ps_mix[0:LO, 0:NS].unsqueeze(2).broadcast_to((LO, NS, SR)), ALU.subtract))
                in_span = Y2[:, 0:NS * SR]
                nc.vector.tensor_copy(rel[:, :], rel_f)
                step(nc.vector.tensor_scalar(in_span, rel_f, 0.0, None, ALU.is_ge))
                step(nc.vector.scalar_tensor_tensor(in_span, rel_f, SPAN - 0.5, in_span, ALU.is_lt, ALU.mult))
                step(nc.vector.tensor_reduce(flags[0:LO, 1:2], in_span, AX.X, ALU.add))
                dve.wait_ge(win_in, 16 * 2 * NB)
                magic = 1.5 * 2.0 ** 23
                step(nc.vector.tensor_copy(lo_f[:, :, :], ws[:, :, :]))
                step(nc.vector.tensor_scalar(hi_f[:, :, :], lo_f[:, :, :], -float(LO // 2), 1.0 / LO, ALU.add, ALU.mult))
                step(nc.vector.tensor_scalar(hi_f[:, :, :], hi_f[:, :, :], magic, None, ALU.add))
                step(nc.vector.tensor_scalar(hi_f[:, :, :], hi_f[:, :, :], magic, None, ALU.subtract))
                step(nc.vector.scalar_tensor_tensor(lo_f[:, :, :], hi_f[:, :, :], -float(LO), lo_f[:, :, :], ALU.mult, ALU.add))
                step(nc.vector.tensor_copy(off[:, :, :], wd[:, :, :]))
                step(nc.vector.tensor_tensor(off[:, :, :], off[:, :, :], limit[:, :].unsqueeze(2).broadcast_to((GROUPS, NB, P)), ALU.subtract))
                step(nc.vector.scalar_tensor_tensor(hi_f[:, :, :], hi_f[:, :, :], float(G), off[:, :, :], ALU.mult, ALU.add))
                step(nc.vector.tensor_scalar(ok[:, :, :], off[:, :, :], 0.0, None, ALU.is_ge))
                step(nc.vector.scalar_tensor_tensor(ok[:, :, :], off[:, :, :], G - 0.5, ok[:, :, :], ALU.is_lt, ALU.mult))
                step(nc.vector.scalar_tensor_tensor(hi_f[:, :, :], hi_f[:, :, :], 1.0, ok[:, :, :], ALU.add, ALU.mult))
                step(nc.vector.tensor_scalar(hi_f[:, :, :], hi_f[:, :, :], -1.0, None, ALU.add))
                dve.sem_inc(c_ok, 1)
                for f in range(G):
                    step(nc.vector.tensor_scalar(ok[:, :, :], off[:, :, :], float(f), None, ALU.is_equal))
                    step(nc.vector.tensor_reduce(cnt[:, :, f], ok[:, :, :], AX.X, ALU.add))
                step(nc.vector.tensor_reduce(flags[0:GROUPS, 0:1], cnt[:, :, :], AX.XY, ALU.add))
                step(nc.vector.tensor_scalar(cnt[:, :, :], cnt[:, :, :], 1.0, None, ALU.max))
                nc.vector.reciprocal(cnt[:, :, :], cnt[:, :, :]).then_inc(cnt_ok, 1)

        A0 = sb("A0", [P, HI * BLOCK], F8)
        A1S = sb("A1S", [P, N + SPAN])
        A1 = A1S[:, 0:N].bitcast(F8)
        rcb = sb("rcb", [P, BLOCK])
        hT_in = sb("hT_in", [D, BLOCK])
        hT_out = sb("hT_out", [D, BLOCK])
        scaled = [sb(f"scaled{i}", [P, BLOCK]) for i in range(2)]
        halves = sb("halves", [LO, SUBS, 2 * D], F16)
        big = sb("big", [LO, SUBS, D])
        top = sb("top", [LO, 2])

        def hold(eng, turns, sem_, value, *more):
            eng.wait_ge(sem_, value)
            for s_, v_ in more:
                eng.wait_ge(s_, v_)
            eng.sem_inc(turns, 1)

        class Node:
            def __init__(self, layer, stack):
                def s(name):
                    return sem(f"{name}{layer}", stack)
                self.summed = [s("summed_a"), s("summed_b")]
                self.scaled = [s("scaled_a"), s("scaled_b")]
                self.in_ = s("node_in")
                self.hT_in = s("hT_in")
                self.mixed, self.acted, self.turned, self.high, self.big, self.low, self.placed, self.stored = (
                    s("mixed"), s("acted"), s("turned"), s("high"), s("big"), s("low"), s("placed"), s("stored"))
                self.step, self.free = s("node_step"), s("free")

        def node_pe_mix(pe, nd, l, j):
            hold(pe, pe_turns, nd.scaled[0], j + 1, (nd.scaled[1], j + 1), (nd.hT_in, 16 * j + 16))
            nc.tensor.matmul(ps_mix[0:D, 0:BLOCK], wl[:, l, :], scaled[0][:, :], start=True, stop=False)
            nc.tensor.matmul(ps_mix[0:D, 0:BLOCK], wl[:, l, :], scaled[1][:, :], start=False, stop=False)
            nc.tensor.matmul(ps_mix[0:D, 0:BLOCK], wr[:, l, :], hT_in[:, :], start=False, stop=True).then_inc(nd.mixed, 1)

        def node_pe_turn(pe, nd, j):
            hold(pe, pe_turns, nd.acted, j + 1)
            for k in range(SUBS):
                last = nc.tensor.transpose(ps_turn[0:LO, D * k:D * (k + 1)], hT_out[:, LO * k:LO * (k + 1)], ident[0:D, 0:D])
            last.then_inc(nd.turned, 1)

        def node_dve_scale(dve, nd, half, j):
            dve.wait_ge(nd.in_, 16 * j + 16)
            dve.wait_ge(nd.summed[half], j + 1)
            nc.vector.tensor_tensor(scaled[half][:, :], ps_S[half][:, 0:BLOCK], rcb[:, :], ALU.mult).then_inc(nd.scaled[half], 1)

        def node_dve_low(dve, nd, j):
            tile = ps_turn[0:LO, 0:SUBS * D].rearrange("p (k d) -> p k d", d=D)
            dve.wait_ge(nd.big, j + 1)
            nc.vector.scalar_tensor_tensor(halves[:, :, D:2 * D], tile, LOW_SCALE, big[:, :, :], ALU.mult, ALU.subtract).then_inc(nd.step, 1)
            nc.vector.tensor_reduce(top[:, 0:1], tile, AX.XY, ALU.max).then_inc(nd.step, 1)
            dve.wait_ge(nd.step, 2 * j + 2)
            nc.vector.tensor_tensor(flags[0:LO, 3:4], flags[0:LO, 3:4], top[:, 0:1], ALU.max).then_inc(nd.low, 1)

        def node_act_relu(act, nd, l, j):
            act.wait_ge(nd.mixed, j + 1)
            act.wait_ge(nd.free, j + 1)
            nc.scalar.activation(hT_out[:, :], ps_mix[0:D, 0:BLOCK], ACT.Relu, bias=biases[:, l:l + 1]).then_inc(nd.acted, 1)

        def node_act_high(act, nd, j):
            act.wait_ge(nd.turned, j + 1)
            act.wait_ge(nd.placed, j + 1)
            nc.scalar.activation(halves[:, :, 0:D], ps_turn[0:LO, 0:SUBS * D].rearrange("p (k d) -> p k d", d=D),
                                 ACT.Copy).then_inc(nd.high, 1)

        def node_pool(pool, nd, l, j):
            hold(pool, pool_turns, nd.high, j + 1)
            nc.gpsimd.tensor_scalar(big[:, :, :], halves[:, :, 0:D], LOW_SCALE, None, ALU.mult).then_inc(nd.big, 1)
            hold(pool, pool_turns, nd.low, j + 1)
            nc.gpsimd.tensor_copy(H[(l + 1) % 2][:, bass.ds(SUBS * j, SUBS), :], halves[:, :, :]).then_inc(nd.placed, 1)

        def node_sp_load(sp, nd, l, j, first=False):
            if not first:
                hold(sp, sp_turns, nd.scaled[0], j, (nd.scaled[1], j), (nd.mixed, j))
            sp.dma_start(rcb[:, :], rcnt_d[0:1, bass.ds(BLOCK * j, BLOCK)].broadcast_to((P, BLOCK))).then_inc(nd.in_, 16)
            sp.dma_start(hT_in[:, :], h_T[l][:, bass.ds(BLOCK * j, BLOCK)]).then_inc(nd.hT_in, 16)

        def node_sp_store(sp, nd, l, j):
            hold(sp, sp_turns, nd.acted, j + 1)
            sp.dma_start(h_T[l + 1][:, bass.ds(BLOCK * j, BLOCK)], hT_out[:, :]).then_inc(nd.stored, 16)
            hold(sp, nd.free, nd.stored, 16 * j + 16)

        with ExitStack() as part:
            iota_c = sb("iota_c", [P, 512], F16, part)
            onehot_c = sb("onehot_c", [P, OH_SLOTS, PAIR, BLOCK], F16, part)
            onehot_l = sb("onehot_l", [P, OH_SLOTS, PAIR, P], F16, part)
            rowsum = sb("rowsum", [P, 2, UNITS], F32, part)
            rowmax = sb("rowmax", [P, NB], F32, part)
            colx = sb("colx", [P, 2, GROUPS], F32, part)

            def bs(name):
                return sem("b_" + name, part)

            iota_ok, onehots, built, evacuated, agged, rows_ok = (
                bs("iota_ok"), bs("onehots"), bs("built"), bs("evacuated"), bs("agged"), bs("rows_ok"))
            a_stored = [bs("a_stored0"), bs("a_stored1")]
            dve_step = bs("dve_step")
            colx_ok = bs("colx_ok")
            nd = Node(0, part)
            A = [A0[:, :], A1]
            block = part.enter_context(nc.Block())

            def turns(eng, body):
                body(0, 0)
                body(1, 1)
                with eng.Fori(1, (NB - 1) // 2) as m:
                    body(m * 2, 0)
                    body(m * 2 + 1, 1)
                for i in range(NB - 1, NB + 2):
                    body(i, i % 2)

            def does(i, lag):
                return 0 <= i - lag < NB if isinstance(i, int) else True

            @block.sync
            def _(sp):
                def body(i, par):
                    if does(i, 1):
                        hold(sp, sp_turns, evacuated, i * UNITS)
                        for c in range(CHUNKS):
                            at = slice(c * CHUNK * BLOCK, (c + 1) * CHUNK * BLOCK)
                            sp.dma_start(matrix[bass.ds(i - 1, 1), :, at].rearrange("o p c -> (o p) c"),
                                         A[1 - par][:, at].bitcast(U8)).then_inc(a_stored[1 - par], 16)
                        node_sp_load(sp, nd, 0, i - 1, first=isinstance(i, int) and i == 1)
                    if does(i, 2):
                        node_sp_store(sp, nd, 0, i - 2)
                turns(sp, body)
                sp.wait_ge(a_stored[0], 16 * CHUNKS * ((NB + 1) // 2))
                sp.wait_ge(a_stored[1], 16 * CHUNKS * (NB // 2))
                sp.wait_ge(nd.stored, 16 * NB)

            @block.gpsimd
            def _(pool):
                nc.gpsimd.iota(iota_c[:, :], pattern=[[1, 512]], base=0, channel_multiplier=0,
                               allow_small_or_imprecise_dtypes=True).then_inc(iota_ok, 1)
                pool.sem_inc(nd.free, 1)
                pool.sem_inc(nd.placed, 1)

                def body(i, par):
                    if does(i, 2):
                        node_pool(pool, nd, 0, i - 2)
                turns(pool, body)

            @block.tensor
            def _(pe):
                def body(i, par):
                    for k in range(UNITS):
                        if does(i, 0):
                            slot = k % OH_SLOTS
                            pe.wait_ge(onehots, i * UNITS + k + 1)
                            if not (isinstance(i, int) and i == 0 and k < PS_SLOTS):
                                pe.wait_ge(evacuated, i * UNITS + k + 1 - PS_SLOTS)
                            for g in range(PAIR):
                                last = nc.tensor.matmul(ps_build[k % PS_SLOTS][:, g, 0:BLOCK], onehot_l[:, slot, g, :],
                                                        onehot_c[:, slot, g, :], start=True, stop=True)
                            last.then_inc(built, 1)
                        if does(i, 1):
                            if k == 0:
                                more = [(nd.scaled[0], i - 1)] if not (isinstance(i, int) and i == 1) else []
                                hold(pe, pe_turns, evacuated, i * UNITS, *more)
                            if k == UNITS // 2 and not (isinstance(i, int) and i == 1):
                                hold(pe, pe_turns, nd.scaled[1], i - 1)
                            half = k // (UNITS // 2)
                            for q in range(2):
                                h = 2 * k + q
                                last = nc.tensor.matmul(ps_S[half][:, 0:BLOCK], H[0][:, h, :], A[1 - par][0:LO, h * BLOCK:(h + 1) * BLOCK],
                                                        start=h % (HI // 2) == 0, stop=h % (HI // 2) == HI // 2 - 1)
                            if k % (UNITS // 2) == UNITS // 2 - 1:
                                last.then_inc(nd.summed[half], 1)
                        if does(i, 2) and k == 8:
                            node_pe_mix(pe, nd, 0, i - 2)
                        if does(i, 2) and k == 16:
                            node_pe_turn(pe, nd, i - 2)
                turns(pe, body)

            @block.scalar
            def _(act):
                def body(i, par):
                    for k in range(UNITS):
                        if does(i, 0):
                            more = []
                            if k == 0 and not (isinstance(i, int) and i < 2):
                                more = [(nd.summed[1], i - 1)]
                                more.append((rows_ok, i - 1))
                                more.append((a_stored[par], (i - par) * (8 * CHUNKS)))
                            hold(act, act_turns, built, i * UNITS + k + 1, *more)
                            to = A[par].rearrange("p (h g f) -> p g h f", h=HI, f=G)[:, PAIR * k:PAIR * (k + 1), :, :]
                            nc.scalar.activation(to, ps_build[k % PS_SLOTS][:, :, 0:BLOCK].rearrange("p g (h f) -> p g h f", f=G),
                                                 ACT.Copy, saturate=True,
                                                 accum_out=rowsum[:, par, k:k + 1]).then_inc(evacuated, 1)
                        if does(i, 2) and k == 10:
                            node_act_relu(act, nd, 0, i - 2)
                        if does(i, 2) and k == 20:
                            node_act_high(act, nd, i - 2)
                turns(act, body)

            @block.vector
            def _(dve):
                dve.wait_ge(iota_ok, 1)

                def body(i, par):
                    if does(i, 0):
                        if not (isinstance(i, int) and i == 0):
                            dve.wait_ge(built, i * UNITS)
                        nc.vector.tensor_copy(colx[:, 0, :], col[:, bass.ds(i * GROUPS, GROUPS)])
                        nc.vector.tensor_copy(colx[:, 1, :], low[:, bass.ds(i * GROUPS, GROUPS)]).then_inc(colx_ok, 1)
                        dve.wait_ge(colx_ok, i + 1)
                    for k in range(UNITS):
                        if does(i, 0):
                            slot = k % OH_SLOTS
                            if not (isinstance(i, int) and i == 0 and k < OH_SLOTS):
                                dve.wait_ge(built, i * UNITS + k + 1 - OH_SLOTS)
                            for g in range(PAIR):
                                at = PAIR * k + g
                                nc.vector.tensor_scalar(onehot_c[:, slot, g, :], iota_c[:, 0:BLOCK], colx[:, 0, at:at + 1], None, ALU.is_equal)
                                last = nc.vector.tensor_scalar(onehot_l[:, slot, g, :], iota_c[:, 0:P], colx[:, 1, at:at + 1], None, ALU.is_equal)
                            last.then_inc(onehots, 1)
                        if does(i, 1) and k == UNITS // 2 + 4:
                            node_dve_scale(dve, nd, 0, i - 1)
                        if does(i, 1) and k == 2:
                            dve.wait_ge(evacuated, i * UNITS)
                            nc.vector.tensor_reduce(rowmax[:, bass.ds(i - 1, 1)], rowsum[:, 1 - par, :], AX.X, ALU.max).then_inc(rows_ok, 1)
                        if does(i, 2) and k == 3:
                            node_dve_scale(dve, nd, 1, i - 2)
                        if does(i, 2) and k == 26:
                            node_dve_low(dve, nd, i - 2)
                turns(dve, body)
                dve.wait_ge(rows_ok, NB)
                nc.vector.tensor_reduce(flags[:, 2:3], rowmax[:, :], AX.X, ALU.max).then_inc(rows_ok, 1)

        def layer(l):
            last_layer = l == LAYERS - 1
            with ExitStack() as part:
                def ls(name):
                    return sem(f"l{l}_{name}", part)

                def lsb(name, shape, dt=F32):
                    return sb(f"l{l}_{name}", shape, dt, part)

                loaded = [ls(f"loaded{c}") for c in range(CHUNKS)]
                nd = Node(l, part)
                consumed = [ls(f"consumed{c}") for c in range(CHUNKS - 1)] + [nd.summed[1]]
                start = ls("start")
                if last_layer:
                    x_in = lsb("x_in", [LO, SUBS, D])
                    x1 = lsb("x1", [LO, SUBS, D])
                    xc = lsb("xc", [LO, SUBS, D])
                    sq = lsb("sq", [LO, SUBS, D])
                    x1b = lsb("x1b", [LO, SUBS, D])
                    result = lsb("result", [LO, SUBS, D])
                    st = lsb("st", [LO, 3, SUBS])
                    agg = lsb("agg", [D, BLOCK])
                    h2T = lsb("h2T", [D, BLOCK])
                    y0 = lsb("y0", [D, BLOCK])
                    y1 = lsb("y1", [D, BLOCK])
                    x_ok, aggd, x1_ok, centred, squared, varied, rooted, normed, turned2, h2_ok = (
                        ls("x_ok"), ls("aggd"), ls("x1_ok"), ls("centred"), ls("squared"), ls("varied"), ls("rooted"),
                        ls("normed"), ls("turned2"), ls("h2_ok"))
                    p0, y0_ok, p1, y1_ok, p2, x1b_ok, out_ok, out_stored, out_free, step = (
                        ls("p0"), ls("y0_ok"), ls("p1"), ls("y1_ok"), ls("p2"), ls("x1b_ok"), ls("out_ok"),
                        ls("out_stored"), ls("out_free"), ls("step"))
                else:
                    iota_s = lsb("iota_s", [P, SPAN])
                    edges = lsb("edges", [LO, 2, SR, D])
                    onehot = lsb("onehot", [LO, 2, SR, SPAN])
                    relx = lsb("relx", [LO, SC * SR])
                    edges_in = [ls("edges_in0"), ls("edges_in1")]
                    hot, esummed, eadded, relx_ok, zeroed = ls("hot"), ls("esummed"), ls("eadded"), ls("relx_ok"), ls("zeroed")
                SE = A1S[0:D, :]
                node_rows = "(b k p) d -> b p k d"
                block = part.enter_context(nc.Block())

                def turns(eng, body):
                    body(0)
                    with eng.Fori(1, NB) as b_:
                        body(b_)
                    body(NB)

                def multiplies(t):
                    return not (isinstance(t, int) and t == NB)

                def has_node(t):
                    return not (isinstance(t, int) and t == 0)

                @block.sync
                def _(sp):
                    def load(t, first):
                        for c in range(CHUNKS):
                            if not first:
                                hold(sp, sp_turns, consumed[c], t)
                            at = slice(c * CHUNK * BLOCK, (c + 1) * CHUNK * BLOCK)
                            sp.dma_start(A0[:, at].bitcast(U8),
                                         matrix[bass.ds(t, 1), :, at].rearrange("o p c -> (o p) c")).then_inc(loaded[c], 16)
                    load(0, True)
                    with sp.Fori(1, NB) as t:
                        load(t, False)

                @block.gpsimd
                def _(pool):
                    if not last_layer:
                        nc.gpsimd.memset(A1S[0:D, :], 0.0).then_inc(zeroed, 1)
                        nc.gpsimd.iota(iota_s[:, :], pattern=[[1, SPAN]], base=0, channel_multiplier=0,
                                       allow_small_or_imprecise_dtypes=True).then_inc(zeroed, 1)
                        pool.sem_inc(nd.free, 1)
                        pool.sem_inc(nd.placed, 1)
                    else:
                        pool.sem_inc(out_free, 1)

                    def body(t):
                        if multiplies(t):
                            if has_node(t):
                                more = [(aggd, t)] if last_layer else []
                                hold(pool, pool_turns, nd.scaled[0], t, (nd.scaled[1], t), (nd.mixed, t), *more)
                            pool.dma_start(rcb[:, :], rcnt_d[0:1, bass.ds(t * BLOCK, BLOCK)].broadcast_to((P, BLOCK))).then_inc(nd.in_, 16)
                            pool.dma_start(hT_in[:, :], h_T[l][:, bass.ds(t * BLOCK, BLOCK)]).then_inc(nd.hT_in, 16)
                            if last_layer:
                                if has_node(t):
                                    hold(pool, pool_turns, x1_ok, t)
                                pool.dma_start(x_in[:, :, :], x.rearrange(node_rows, k=SUBS, p=LO)[bass.ds(t, 1), :, :, :]
                                               .rearrange("o p k d -> (o p) k d")).then_inc(x_ok, 16)
                        if has_node(t) and not last_layer:
                            hold(pool, pool_turns, nd.acted, t)
                            pool.dma_start(h_T[l + 1][:, bass.ds((t - 1) * BLOCK, BLOCK)], hT_out[:, :]).then_inc(nd.stored, 16)
                            hold(pool, nd.free, nd.stored, t * 16)
                            node_pool(pool, nd, l, t - 1)
                        if has_node(t) and last_layer:
                            hold(pool, pool_turns, x1_ok, t)
                            nc.gpsimd.tensor_tensor(x1b[:, :, :], x1[:, :, :], b2_bc[:, :, :], ALU.add).then_inc(x1b_ok, 1)
                            hold(pool, pool_turns, out_ok, t)
                            pool.dma_start(out.rearrange(node_rows, k=SUBS, p=LO)[bass.ds(t - 1, 1), :, :, :]
                                           .rearrange("o p k d -> (o p) k d"), result[:, :, :]).then_inc(out_stored, 16)
                            hold(pool, out_free, out_stored, t * 16)
                    turns(pool, body)
                    if last_layer:
                        pool.wait_ge(out_stored, 16 * NB)
                    else:
                        pool.wait_ge(nd.stored, 16 * NB)

                def superchunk(pe, t, k):
                    slot = k % 2
                    waits = [(edges_in[slot], (t * (SC // 2) + k // 2 + 1) * 32)]
                    if not (isinstance(t, int) and t == 0 and k < 2):
                        waits.append((eadded, t * SC + k - 1))
                    hold(pe, pe_turns, hot, t * SC + k + 1, *waits)
                    for r in range(SR):
                        last = nc.tensor.matmul(ps_build[slot][0:D, 0, 0:SPAN], edges[:, slot, r, :], onehot[:, slot, r, :],
                                                start=r == 0, stop=r == SR - 1)
                    last.then_inc(esummed, 1)

                @block.tensor
                def _(pe):
                    def body(t):
                        for h in range(HI):
                            half, c = h // (HI // 2), h // CHUNK
                            if multiplies(t):
                                if h % (HI // 2) == 0 and has_node(t):
                                    hold(pe, pe_turns, nd.scaled[half], t)
                                if h % CHUNK == 0:
                                    hold(pe, pe_turns, loaded[c], t * 16 + 16)
                                last = nc.tensor.matmul(ps_S[half][:, 0:BLOCK], H[l % 2][:, h, :], A0[0:LO, h * BLOCK:(h + 1) * BLOCK],
                                                        start=h % (HI // 2) == 0, stop=h % (HI // 2) == HI // 2 - 1)
                                if h % CHUNK == CHUNK - 1 and h < HI - 1:
                                    last.then_inc(consumed[c], 1)
                                if h % (HI // 2) == HI // 2 - 1:
                                    last.then_inc(nd.summed[half], 1)
                                if not last_layer and h % 25 == 20:
                                    superchunk(pe, t, h // 25)
                            if not has_node(t):
                                continue
                            j = t - 1
                            if h == 4:
                                node_pe_mix(pe, nd, l, j)
                            if h == 14 and not last_layer:
                                node_pe_turn(pe, nd, j)
                            if last_layer:
                                if h == 14:
                                    node_pe_turn(pe, nd, j)
                                if h == 40:
                                    hold(pe, pe_turns, normed, t)
                                    for k in range(SUBS):
                                        last2 = nc.tensor.transpose(ps_mix[0:D, LO * k:LO * (k + 1)], xc[:, k, :], ident[0:LO, 0:LO])
                                    last2.then_inc(turned2, 1)
                                if h == 52:
                                    hold(pe, pe_turns, h2_ok, t, (aggd, t))
                                    nc.tensor.matmul(ps_build[0][0:D, 0, 0:BLOCK], w0a[:, :], agg[:, :], start=True, stop=False)
                                    nc.tensor.matmul(ps_build[0][0:D, 0, 0:BLOCK], w0v[:, :], h2T[:, :], start=False, stop=True).then_inc(p0, 1)
                                if h == 64:
                                    hold(pe, pe_turns, y0_ok, t)
                                    nc.tensor.matmul(ps_build[0][0:D, 1, 0:BLOCK], w1[:, :], y0[:, :], start=True, stop=True).then_inc(p1, 1)
                                if h == 76:
                                    hold(pe, pe_turns, y1_ok, t)
                                    for k in range(SUBS):
                                        last2 = nc.tensor.matmul(ps_build[1][0:LO, 0, D * k:D * (k + 1)], y1[:, LO * k:LO * (k + 1)], w2[:, :],
                                                                 start=True, stop=True)
                                    last2.then_inc(p2, 1)
                    turns(pe, body)

                @block.scalar
                def _(act):
                    def body(t):
                        if multiplies(t) and not last_layer:
                            for k in range(SC):
                                slot = k % 2
                                if not (isinstance(t, int) and t == 0 and k < 2):
                                    act.wait_ge(esummed, t * SC + k - 1)
                                rows_ = attr.rearrange("(s p r) d -> s p r d", p=LO, r=SR)[bass.ds(t * SC + k, 1), :, :, :].rearrange("o p r d -> (o p) r d")
                                act.dma_start(edges[0:DMA_P, slot, :, :], rows_[0:DMA_P, :, :]).then_inc(edges_in[slot], 16)
                                act.dma_start(edges[DMA_P:LO, slot, :, :], rows_[DMA_P:LO, :, :]).then_inc(edges_in[slot], 16)
                                if has_node(t):
                                    if k == 1:
                                        node_act_relu(act, nd, l, t - 1)
                                    if k == 2:
                                        node_act_high(act, nd, t - 1)
                        elif not last_layer:
                            node_act_relu(act, nd, l, t - 1)
                            node_act_high(act, nd, t - 1)
                        if has_node(t) and last_layer:
                            act.wait_ge(nd.mixed, t)
                            nc.scalar.activation(hT_out[:, :], ps_mix[0:D, 0:BLOCK], ACT.Identity, bias=biases[:, l:l + 1]).then_inc(nd.acted, 1)
                            act.wait_ge(centred, t)
                            nc.scalar.activation(sq[:, :, :], xc[:, :, :], ACT.Square).then_inc(squared, 1)
                            act.wait_ge(varied, t)
                            nc.scalar.activation(st[:, 1, :], st[:, 1, :], ACT.Sqrt).then_inc(rooted, 1)
                            act.wait_ge(turned2, t)
                            nc.scalar.activation(h2T[:, :], ps_mix[0:D, 0:BLOCK], ACT.Relu).then_inc(h2_ok, 1)
                            act.wait_ge(p0, t)
                            nc.scalar.activation(y0[:, :], ps_build[0][0:D, 0, 0:BLOCK], ACT.Relu, bias=biases[:, LAYERS:LAYERS + 1]).then_inc(y0_ok, 1)
                            act.wait_ge(p1, t)
                            nc.scalar.activation(y1[:, :], ps_build[0][0:D, 1, 0:BLOCK], ACT.Relu,
                                                 bias=biases[:, LAYERS + 1:LAYERS + 2]).then_inc(y1_ok, 1)
                    turns(act, body)

                @block.vector
                def _(dve):
                    def hots(t, k):
                        if not (isinstance(t, int) and t == 0 and k < 2):
                            dve.wait_ge(esummed, t * SC + k - 1)
                        for r in range(SR):
                            last = nc.vector.tensor_scalar(onehot[:, k % 2, r, :], iota_s[0:LO, :], relx[:, k * SR + r:k * SR + r + 1],
                                                           None, ALU.is_equal)
                        last.then_inc(hot, 1)

                    def add(t, k):
                        base = dve.value_load(base_i[0:1, bass.ds(t * SC + k, 1)], min_val=0, max_val=N - 1)
                        at = SE[:, bass.ds(base, SPAN)]
                        dve.wait_ge(esummed, t * SC + k + 1)
                        nc.vector.tensor_tensor(at, at, ps_build[k % 2][0:D, 0, 0:SPAN], ALU.add).then_inc(eadded, 1)
                        dve.wait_ge(eadded, t * SC + k + 1)

                    if not last_layer:
                        dve.wait_ge(zeroed, 2)

                    def steps(t, n, ins):
                        ins.then_inc(step, 1)
                        dve.wait_ge(step, (t - 1) * 5 + n)

                    def body(t):
                        if has_node(t):
                            node_dve_scale(dve, nd, 1, t - 1)
                        if has_node(t) and last_layer:
                            if not (isinstance(t, int) and t == 1):
                                pass
                            nc.vector.tensor_tensor(agg[:, :], SE[:, bass.ds((t - 1) * BLOCK, BLOCK)], rcb[0:D, :], ALU.mult).then_inc(aggd, 1)
                            wide = (LO, SUBS, D)
                            dve.wait_ge(nd.turned, t)
                            dve.wait_ge(x_ok, t * 16)
                            nc.vector.tensor_tensor(x1[:, :, :], ps_turn[0:LO, 0:SUBS * D].rearrange("p (k d) -> p k d", d=D),
                                                    x_in[:, :, :], ALU.add).then_inc(x1_ok, 1)
                            dve.wait_ge(x1_ok, t)
                            steps(t, 1, nc.vector.tensor_reduce(st[:, 0, :], x1[:, :, :], AX.X, ALU.add))
                            steps(t, 2, nc.vector.tensor_scalar(st[:, 0, :], st[:, 0, :], 1.0 / D, None, ALU.mult))
                            nc.vector.tensor_tensor(xc[:, :, :], x1[:, :, :], st[:, 0, :].unsqueeze(2).broadcast_to(wide),
                                                    ALU.subtract).then_inc(centred, 1)
                            dve.wait_ge(squared, t)
                            steps(t, 3, nc.vector.tensor_reduce(st[:, 1, :], sq[:, :, :], AX.X, ALU.add))
                            nc.vector.tensor_scalar(st[:, 1, :], st[:, 1, :], 1.0 / D, EPS, ALU.mult, ALU.add).then_inc(varied, 1)
                            dve.wait_ge(rooted, t)
                            steps(t, 4, nc.vector.reciprocal(st[:, 2, :], st[:, 1, :]))
                            nc.vector.tensor_tensor(xc[:, :, :], xc[:, :, :], st[:, 2, :].unsqueeze(2).broadcast_to(wide),
                                                    ALU.mult).then_inc(normed, 1)
                        if multiplies(t) and not last_layer:
                            if has_node(t):
                                dve.wait_ge(esummed, t * SC)
                            nc.vector.tensor_copy(relx[:, :], rel[:, bass.ds(t * (SC * SR), SC * SR)]).then_inc(relx_ok, 1)
                            dve.wait_ge(relx_ok, t + 1)
                            hots(t, 0)
                            hots(t, 1)
                            add(t, 0)
                            if has_node(t):
                                node_dve_low(dve, nd, t - 1)
                            hots(t, 2)
                            node_dve_scale(dve, nd, 0, t)
                            add(t, 1)
                            hots(t, 3)
                            add(t, 2)
                            add(t, 3)
                        elif not last_layer:
                            node_dve_low(dve, nd, t - 1)
                        if multiplies(t) and last_layer:
                            node_dve_scale(dve, nd, 0, t)
                        if has_node(t) and last_layer:
                            dve.wait_ge(x1b_ok, t)
                            dve.wait_ge(p2, t)
                            dve.wait_ge(out_free, t)
                            nc.vector.tensor_tensor(result[:, :, :], ps_build[1][0:LO, 0, 0:SUBS * D].rearrange("p (k d) -> p k d", d=D),
                                                    x1b[:, :, :], ALU.add).then_inc(out_ok, 1)
                            steps(t, 5, nc.vector.tensor_copy(st[:, 2, 0:1], st[:, 2, 1:2]))
                    turns(dve, body)

        for l in range(1, LAYERS):
            layer(l)

        with ExitStack() as part:
            ones_c = sb("ones_c", [P, 1], F32, part)
            tests = sb("tests", [P, 4], F32, part)
            sums = sb("sums", [1, 4], F32, part)
            set_, tested, added, step = sem("v_set", part), sem("v_tested", part), sem("v_added", part), sem("v_step", part)
            block = part.enter_context(nc.Block())

            @block.gpsimd
            def _(pool):
                nc.gpsimd.memset(ones_c[:, :], 1.0).then_inc(set_, 1)

            @block.tensor
            def _(pe):
                pe.wait_ge(set_, 1)
                pe.wait_ge(tested, 1)
                nc.tensor.matmul(ps_mix[0:1, 0:4], ones_c[:, :], tests[:, :], start=True, stop=True).then_inc(added, 1)

            @block.vector
            def _(dve):
                nc.vector.tensor_copy(tests[:, 0:2], flags[:, 0:2]).then_inc(step, 1)
                nc.vector.tensor_scalar(tests[:, 2:3], flags[:, 2:3], MAX_COUNT, None, ALU.is_gt).then_inc(step, 1)
                nc.vector.tensor_scalar(tests[:, 3:4], flags[:, 3:4], MAX_H, None, ALU.is_gt).then_inc(tested, 1)
                dve.wait_ge(added, 1)
                nc.vector.tensor_scalar(sums[:, 0:2], ps_mix[0:1, 0:2], float(E), None, ALU.not_equal).then_inc(step, 1)
                nc.vector.tensor_scalar(sums[:, 2:4], ps_mix[0:1, 2:4], 0.5, None, ALU.is_gt).then_inc(step, 1)
                dve.wait_ge(step, 4)
                nc.vector.tensor_reduce(verdict[0:1, 0:1], sums[:, :], AX.X, ALU.max).then_inc(step, 1)
                dve.wait_ge(step, 5)


def general_path(nc, x, src, dst, attr, Wl, Wr, b, W0, b0, W1, b1, W2, b2, out):
    with ExitStack() as ctx:
        def sb(name, shape, dt=F32):
            return ctx.enter_context(nc.sbuf_tensor("g_" + name, shape, dt))

        def pb(name, shape, dt=F32):
            return ctx.enter_context(nc.psum_tensor("g_" + name, shape, dt))

        def sem(name):
            return ctx.enter_context(nc.semaphore("g_" + name))

        table = nc.dram_tensor("g_table", (N, D), F32).ap()
        sums = [nc.dram_tensor(f"g_sums{i}", (N + GP, D + 1), F32).ap() for i in range(LAYERS + 1)]
        by_part = "(p t) d -> p t d"

        X = sb("X", [GP, GT, D])
        H = sb("H", [GP, GT, D])
        S = sb("S", [GP, GT, D + 1])
        rcnt = sb("rcnt", [GP, GT])
        stat = sb("stat", [GP, 2, GT])
        src_i = sb("src_i", [GP, GE], I32)
        dst_i = sb("dst_i", [GP, GE], I32)
        ident = sb("ident", [GP, GP])
        earlier = sb("earlier", [GP, GP])
        eq = sb("eq", [GP, GP])
        eqe = sb("eqe", [GP, GP])
        dcol = sb("dcol", [GP, 1])
        dup = sb("dup", [GP, 1])
        spare = sb("spare", [GP, 1])
        at_src = sb("at_src", [GP, 1], I32)
        at_dst = sb("at_dst", [GP, 1], I32)
        msg = sb("msg", [GP, D + 1])
        comb = sb("comb", [GP, D + 1])
        cat = sb("cat", [GP, 2 * D])
        catT = sb("catT", [2 * D, GP])
        y0 = sb("y0", [D, GP])
        y1 = sb("y1", [D, GP])
        w = sb("w", [2 * D, LAYERS, D])
        w0 = sb("w0", [2 * D, D])
        w1 = sb("w1", [D, D])
        w2 = sb("w2", [D, D])
        bias = sb("bias", [GP, LAYERS + 1, D])
        bias01 = sb("bias01", [D, 2])
        ps_dst = pb("ps_dst", [GP, GP])
        ps_comb = pb("ps_comb", [GP, D + 1])
        ps_T = pb("ps_T", [2 * D, GP])
        ps_a = pb("ps_a", [GP, D])
        ps_y0 = pb("ps_y0", [D, GP])
        ps_y1 = pb("ps_y1", [D, GP])

        loaded = sem("loaded")
        constants = sem("constants")
        const_step = sem("const_step")

        def layernorm_relu(steps, of, to):
            m, v = stat[:, 0, :], stat[:, 1, :]
            wide = (GP, GT, D)
            steps(nc.vector.tensor_reduce(m, of, AX.X, ALU.add))
            steps(nc.vector.tensor_scalar(m, m, 1.0 / D, None, ALU.mult))
            steps(nc.vector.tensor_tensor(to, of, m.unsqueeze(2).broadcast_to(wide), ALU.subtract))
            steps(nc.vector.tensor_tensor(S[:, :, 0:D], to, to, ALU.mult))
            steps(nc.vector.tensor_reduce(v, S[:, :, 0:D], AX.X, ALU.add))
            steps(nc.vector.tensor_scalar(v, v, 1.0 / D, EPS, ALU.mult, ALU.add))

        with ExitStack() as part:
            varied = part.enter_context(nc.semaphore("g_varied"))
            rooted = part.enter_context(nc.semaphore("g_rooted"))
            dve_step = part.enter_context(nc.semaphore("g_dve_step0"))
            zeroed = part.enter_context(nc.semaphore("g_zeroed"))
            normed = part.enter_context(nc.semaphore("g_normed"))
            stored = part.enter_context(nc.semaphore("g_stored0"))
            block = part.enter_context(nc.Block())

            @block.sync
            def _(sp):
                sp.dma_start(X[:, :, :], x.rearrange(by_part, p=GP)).then_inc(loaded, 16)
                sp.dma_start(src_i[:, :], src.rearrange("(p j) -> p j", p=GP)).then_inc(loaded, 16)
                sp.dma_start(dst_i[:, :], dst.rearrange("(p j) -> p j", p=GP)).then_inc(loaded, 16)
                sp.dma_start(w[0:D, :, :], Wl.rearrange("l i o -> i l o")).then_inc(loaded, 16)
                sp.dma_start(w[D:2 * D, :, :], Wr.rearrange("l i o -> i l o")).then_inc(loaded, 16)
                sp.dma_start(w0[:, :], W0).then_inc(loaded, 16)
                sp.dma_start(w1[:, :], W1).then_inc(loaded, 16)
                sp.dma_start(w2[:, :], W2).then_inc(loaded, 16)
                for i in range(LAYERS):
                    sp.dma_start(bias[:, i, :], b[i:i + 1, :].broadcast_to((GP, D))).then_inc(loaded, 16)
                sp.dma_start(bias[:, LAYERS, :], b2.unsqueeze(0).broadcast_to((GP, D))).then_inc(loaded, 16)
                sp.dma_start(bias01[:, 0:1], b0.unsqueeze(1)).then_inc(loaded, 16)
                sp.dma_start(bias01[:, 1:2], b1.unsqueeze(1)).then_inc(loaded, 16)
                sp.wait_ge(zeroed, 1)
                for i in range(LAYERS + 1):
                    sp.dma_start(sums[i][0:N, :].rearrange(by_part, p=GP), S[:, :, :]).then_inc(stored, 16)
                    sp.dma_start(sums[i][N:N + GP, :], S[:, 0, :]).then_inc(stored, 16)
                sp.wait_ge(normed, 1)
                sp.dma_start(table.rearrange(by_part, p=GP), H[:, :, :]).then_inc(stored, 16)
                sp.wait_ge(stored, 16 * (2 * LAYERS + 3))
                sp.wait_ge(loaded, 16 * 14)

            @block.gpsimd
            def _(pool):
                nc.gpsimd.memset(ident[:, :], 0.0).then_inc(const_step, 1)
                nc.gpsimd.memset(earlier[:, :], 1.0).then_inc(const_step, 1)
                pool.wait_ge(const_step, 2)
                nc.gpsimd.affine_select(out=ident[:, :], in_=ident[:, :], compare_op=ALU.not_equal, fill=1.0,
                                        base=0, pattern=[[-1, GP]], channel_multiplier=1).then_inc(constants, 1)
                nc.gpsimd.affine_select(out=earlier[:, :], in_=earlier[:, :], compare_op=ALU.is_gt, fill=0.0,
                                        base=0, pattern=[[-1, GP]], channel_multiplier=1).then_inc(constants, 1)
                nc.gpsimd.memset(msg[:, :], 1.0).then_inc(constants, 1)
                nc.gpsimd.iota(spare[:, :], pattern=[[0, 1]], base=N, channel_multiplier=1,
                               allow_small_or_imprecise_dtypes=True).then_inc(constants, 1)

            @block.scalar
            def _(act):
                act.wait_ge(varied, 1)
                nc.scalar.activation(stat[:, 1, :], stat[:, 1, :], ACT.Sqrt).then_inc(rooted, 1)

            @block.tensor
            def _(pe):
                pe.wait_ge(constants, 4)

            @block.vector
            def _(dve):
                count = [0]

                def steps(ins):
                    count[0] += 1
                    ins.then_inc(dve_step, 1)
                    dve.wait_ge(dve_step, count[0])

                nc.vector.memset(S[:, :, :], 0.0).then_inc(zeroed, 1)
                dve.wait_ge(loaded, 16 * 14)
                dve.wait_ge(stored, 16 * (2 * LAYERS + 2))
                layernorm_relu(steps, X[:, :, :], H[:, :, :])
                nc.vector.tensor_copy(stat[:, 0, :], stat[:, 0, :]).then_inc(varied, 1)
                dve.wait_ge(rooted, 1)
                steps(nc.vector.reciprocal(stat[:, 1, :], stat[:, 1, :]))
                steps(nc.vector.tensor_tensor(H[:, :, :], H[:, :, :],
                                              stat[:, 1, :].unsqueeze(2).broadcast_to((GP, GT, D)), ALU.mult))
                nc.vector.tensor_scalar(H[:, :, :], H[:, :, :], 0.0, None, ALU.max).then_inc(normed, 1)

        def edge_block(i):
            with ExitStack() as part:
                def s(name):
                    return part.enter_context(nc.semaphore(f"g_{name}{i}"))

                turns, indexed, transposed, equal, summed, ready = s("turns"), s("indexed"), s("transposed"), s("equal"), s("summed"), s("ready")
                gathered, scattered, dve_step = s("gathered"), s("scattered"), s("dve_step")
                block = part.enter_context(nc.Block())

                @block.gpsimd
                def _(pool):
                    with pool.Fori(0, GE) as j:
                        pool.wait_ge(indexed, j + 1)
                        pool.sem_inc(turns, 1)
                        if i < LAYERS:
                            nc.gpsimd.indirect_dma_start(
                                out=msg[:, 0:D], out_offset=None, in_=table[:, :],
                                in_offset=bass.IndirectOffsetOnAxis(ap=at_src[:, 0:1], axis=0)).then_inc(gathered, 16)
                        else:
                            pool.dma_start(msg[:, 0:D],
                                           attr.rearrange("(p j) d -> p j d", p=GP)[:, bass.ds(j, 1), :]
                                           .rearrange("p j d -> p (j d)")).then_inc(gathered, 16)
                        pool.wait_ge(ready, j + 1)
                        pool.sem_inc(turns, 1)
                        nc.gpsimd.indirect_dma_start(
                            out=sums[i][:, :], out_offset=bass.IndirectOffsetOnAxis(ap=at_dst[:, 0:1], axis=0),
                            in_=comb[:, :], in_offset=None,
                            compute_op=ALU.add).then_inc(scattered, 16)
                        pool.wait_ge(scattered, 16 * j + 16)

                @block.tensor
                def _(pe):
                    with pe.Fori(0, GE) as j:
                        pe.wait_ge(indexed, j + 1)
                        nc.tensor.transpose(ps_dst[:, :], dcol[:, 0:1].broadcast_to((GP, GP)), ident[:, :]).then_inc(transposed, 1)
                        pe.wait_ge(equal, j + 1)
                        pe.wait_ge(gathered, 16 * j + 16)
                        nc.tensor.matmul(ps_comb[:, :], eq[:, :], msg[:, :], start=True, stop=True).then_inc(summed, 1)

                @block.vector
                def _(dve):
                    with dve.Fori(0, GE) as j:
                        def step(ins, k):
                            ins.then_inc(dve_step, 1)
                            dve.wait_ge(dve_step, 6 * j + k)

                        step(nc.vector.tensor_copy(at_src[:, :], src_i[:, bass.ds(j, 1)]), 1)
                        nc.vector.tensor_copy(dcol[:, :], dst_i[:, bass.ds(j, 1)]).then_inc(indexed, 1)
                        dve.wait_ge(transposed, j + 1)
                        step(nc.vector.tensor_scalar(eq[:, :], ps_dst[:, :], dcol[:, 0:1], None, ALU.is_equal), 2)
                        step(nc.vector.tensor_tensor(eqe[:, :], eq[:, :], earlier[:, :], ALU.mult), 3)
                        step(nc.vector.tensor_reduce(dup[:, :], eqe[:, :], AX.X, ALU.max), 4)
                        step(nc.vector.tensor_scalar(dup[:, :], spare[:, :], dcol[:, 0:1], dup[:, 0:1],
                                                     ALU.subtract, ALU.mult), 5)
                        nc.vector.tensor_tensor(at_dst[:, :], dup[:, :], dcol[:, :], ALU.add).then_inc(equal, 1)
                        dve.wait_ge(summed, j + 1)
                        step(nc.vector.tensor_copy(comb[:, :], ps_comb[:, :]), 6)
                        nc.vector.tensor_copy(dup[:, :], dup[:, :]).then_inc(ready, 1)
                        dve.wait_ge(scattered, 16 * j + 16)

        def node_block(i):
            last = i == LAYERS
            with ExitStack() as part:
                def s(name):
                    return part.enter_context(nc.semaphore(f"g_{name}n{i}"))

                landed, joined, turned, turned_sb, mixed = s("landed"), s("joined"), s("turned"), s("turned_sb"), s("mixed")
                y0_ps, y0_sb, y1_ps, y1_sb, done, stored, dve_step = (
                    s("y0_ps"), s("y0_sb"), s("y1_ps"), s("y1_sb"), s("done"), s("stored"), s("dve_step"))
                varied, rooted = s("varied"), s("rooted")
                block = part.enter_context(nc.Block())
                to_dram = out if last else table

                @block.sync
                def _(sp):
                    sp.dma_start(S[:, :, :], sums[i][0:N, :].rearrange(by_part, p=GP)).then_inc(landed, 16)
                    if i == LAYERS - 1:
                        return
                    sp.wait_ge(done, 1)
                    sp.dma_start(to_dram.rearrange(by_part, p=GP), (X if last else H)[:, :, :]).then_inc(stored, 16)
                    sp.wait_ge(stored, 16)

                @block.tensor
                def _(pe):
                    with pe.Fori(0, GT) as t:
                        pe.wait_ge(joined, t + 1)
                        nc.tensor.transpose(ps_T[:, :], cat[:, :], ident[:, :]).then_inc(turned, 1)
                        pe.wait_ge(turned_sb, t + 1)
                        if not last:
                            nc.tensor.matmul(ps_a[:, :], catT[:, :], w[:, i, :], start=True, stop=True).then_inc(mixed, 1)
                        else:
                            nc.tensor.matmul(ps_y0[:, :], w0[:, :], catT[:, :], start=True, stop=True).then_inc(y0_ps, 1)
                            pe.wait_ge(constants, 4)
                            pe.wait_ge(y0_sb, t + 1)
                            nc.tensor.matmul(ps_y1[:, :], w1[:, :], y0[:, :], start=True, stop=True).then_inc(y1_ps, 1)
                            pe.wait_ge(constants, 4)
                            pe.wait_ge(y1_sb, t + 1)
                            nc.tensor.matmul(ps_a[:, :], y1[:, :], w2[:, :], start=True, stop=True).then_inc(mixed, 1)

                @block.scalar
                def _(act):
                    if last:
                        with act.Fori(0, GT) as t:
                            act.wait_ge(y0_ps, t + 1)
                            nc.scalar.activation(y0[:, :], ps_y0[:, :], ACT.Relu, bias=bias01[:, 0:1]).then_inc(y0_sb, 1)
                            act.wait_ge(y1_ps, t + 1)
                            nc.scalar.activation(y1[:, :], ps_y1[:, :], ACT.Relu, bias=bias01[:, 1:2]).then_inc(y1_sb, 1)
                    if i == LAYERS - 1:
                        act.wait_ge(varied, 1)
                        nc.scalar.activation(stat[:, 1, :], stat[:, 1, :], ACT.Sqrt).then_inc(rooted, 1)

                @block.vector
                def _(dve):
                    dve.wait_ge(landed, 16)
                    nc.vector.tensor_scalar(rcnt[:, :], S[:, :, D], 1.0, None, ALU.max).then_inc(dve_step, 1)
                    dve.wait_ge(dve_step, 1)
                    nc.vector.reciprocal(rcnt[:, :], rcnt[:, :]).then_inc(dve_step, 1)
                    dve.wait_ge(dve_step, 2)
                    with dve.Fori(0, GT) as t:
                        def step(ins, k):
                            ins.then_inc(dve_step, 1)
                            dve.wait_ge(dve_step, 3 * t + 2 + k)

                        def row(a):
                            return a[:, bass.ds(t, 1), 0:D].rearrange("p t d -> p (t d)")

                        step(nc.vector.tensor_scalar(cat[:, 0:D], row(S), rcnt[:, bass.ds(t, 1)], None, ALU.mult), 1)
                        nc.vector.tensor_copy(cat[:, D:2 * D], row(H)).then_inc(joined, 1)
                        dve.wait_ge(turned, t + 1)
                        nc.vector.tensor_copy(catT[:, :], ps_T[:, :]).then_inc(turned_sb, 1)
                        dve.wait_ge(mixed, t + 1)
                        if i < LAYERS - 1:
                            step(nc.vector.tensor_tensor(row(H), ps_a[:, :], bias[:, i, :], ALU.add), 2)
                            step(nc.vector.tensor_scalar(row(H), row(H), 0.0, None, ALU.max), 3)
                        else:
                            step(nc.vector.tensor_tensor(row(H), ps_a[:, :], bias[:, i, :], ALU.add), 2)
                            step(nc.vector.tensor_tensor(row(X), row(H), row(X), ALU.add), 3)
                    count = [3 * GT + 2]

                    def steps(ins):
                        count[0] += 1
                        ins.then_inc(dve_step, 1)
                        dve.wait_ge(dve_step, count[0])

                    if i == LAYERS - 1:
                        layernorm_relu(steps, X[:, :, :], H[:, :, :])
                        nc.vector.tensor_copy(stat[:, 0, :], stat[:, 0, :]).then_inc(varied, 1)
                        dve.wait_ge(rooted, 1)
                        steps(nc.vector.reciprocal(stat[:, 1, :], stat[:, 1, :]))
                        steps(nc.vector.tensor_tensor(H[:, :, :], H[:, :, :],
                                                      stat[:, 1, :].unsqueeze(2).broadcast_to((GP, GT, D)), ALU.mult))
                        steps(nc.vector.tensor_scalar(H[:, :, :], H[:, :, :], 0.0, None, ALU.max))
                    nc.vector.tensor_copy(rcnt[:, :], rcnt[:, :]).then_inc(done, 1)

        for i in range(LAYERS + 1):
            edge_block(i)
            node_block(i)


def both_paths(nc, *args):
    with ExitStack() as ctx:
        verdict = ctx.enter_context(nc.sbuf_tensor("verdict", [1, 1], I32))
        dense_path(nc, *args, verdict)
        refused = nc.values_load(verdict[0:1, 0:1], min_val=0, max_val=1)
        with nc.If(refused > 0):
            general_path(nc, *args)


_INS = ['x', 'src', 'dst', 'edge_attr_64', 'L0_gnn_Wl', 'L0_gnn_Wr', 'L0_gnn_b', 'L1_gnn_W0', 'L1_gnn_b0',
        'L1_gnn_W1', 'L1_gnn_b1', 'L1_gnn_W2', 'L1_gnn_b2']


def kernel(**inputs):
    import numpy as _np
    import concourse.bacc as _bacc
    from concourse import mybir as _mybir
    from concourse.bass_utils import run_bass_kernel_spmd as _run

    nc = _bacc.Bacc("TRN2", target_bir_lowering=False, num_devices=1)
    arrays, args = {}, []
    for name in _INS:
        a = _np.ascontiguousarray(inputs[name])
        arrays[f"in_{name}"] = a
        args.append(nc.dram_tensor(f"in_{name}", a.shape, _mybir.dt.from_np(a.dtype), kind="ExternalInput").ap())
    out = nc.dram_tensor("out_0", (N, D), _mybir.dt.float32, kind="ExternalOutput").ap()
    both_paths(nc, *args, out)
    r = _run(nc, [arrays], core_ids=[0])
    return r.results[0]["out_0"]
```

```python
from contextlib import ExitStack

import concourse.bass as bass
from concourse import mybir

F32 = mybir.dt.float32
F16 = mybir.dt.float16
F8 = mybir.dt.float8e4
I32 = mybir.dt.int32
U8 = mybir.dt.uint8
ALU = mybir.AluOpType
ACT = mybir.ActivationFunctionType
AX = mybir.AxisListType

N = 12500
E = 212500
D = 64
LAYERS = 3
EPS = 1e-5
GP = 125
GT = N // GP
GE = E // GP

P = 128
LO = 125
HI = N // LO
G = 5
BLOCK = 500
NB = N // BLOCK
GROUPS = BLOCK // G
COLS = (HI + 1) * G
SUBS = BLOCK // LO
PAIR = 2
UNITS = GROUPS // PAIR
OH_SLOTS = 5
POOL_SLOT = 4
PS_SLOTS = 2
ROW = 425
ROWS = E // ROW
COUNT_BITS = 87.5
LOW_SCALE = 2048.0
MAX_H = 60000.0
CHUNKS = 5
CHUNK = HI // CHUNKS
SC = 4
SR = 17
NS = NB * SC
SPAN = 152
DMA_P = 112
assert LO * SR * NS == E and GROUPS * G * NB == N and ROW * ROWS == E


def dense_path(nc, x, src, dst, attr, Wl, Wr, b, W0, b0, W1, b1, W2, b2, out, verdict, used, kept):
    with ExitStack() as ctx:
        def sb(name, shape, dt=F32, stack=ctx):
            return stack.enter_context(nc.sbuf_tensor(name, shape, dt))

        def pb(name, shape, dt=F32, stack=ctx):
            return stack.enter_context(nc.psum_tensor(name, shape, dt))

        def sem(name, stack=ctx):
            used.append(stack.enter_context(nc.semaphore(name)))
            return used[-1]

        def pool_dma_sem(name):
            return kept.enter_context(nc.semaphore(name))

        matrix = nc.dram_tensor("matrix", (NB, P, HI * BLOCK), U8).ap()
        h_T = [nc.dram_tensor(f"h_T{i}", (D, N), F32).ap() for i in range(LAYERS)]
        rcnt_d = nc.dram_tensor("rcnt_d", (1, N), F32).ap()

        H = [sb(f"H{i}", [LO, HI, 2 * D], F16) for i in range(2)]
        low = sb("low", [P, GROUPS * NB], F16)
        col = sb("col", [P, GROUPS * NB], F16)
        rel = sb("rel", [LO, NS * SR], F16)
        base_i = sb("base_i", [1, NS], I32)
        ident = sb("ident", [P, P])
        wl = sb("wl", [P, LAYERS, D])
        wr = sb("wr", [D + 1, LAYERS, D])
        w0a = sb("w0a", [P, D])
        w0v = sb("w0v", [D, D])
        w1 = sb("w1", [D, D])
        w2 = sb("w2", [D, D])
        b01 = sb("b01", [D, 2])
        b2_bc = sb("b2_bc", [LO, SUBS, D])
        flags = sb("flags", [P, 4])

        ps_build = [pb(f"ps_build{i}", [P, PAIR, 512]) for i in range(PS_SLOTS)]
        ps_S = [pb(f"ps_S{i}", [P, 512]) for i in range(2)]
        ps_mix = pb("ps_mix", [P, 512])
        ps_turn = pb("ps_turn", [P, 512])

        constants = sem("constants")
        sp_turns, act_turns, pe_turns, pool_turns = sem("sp_turns"), sem("act_turns"), sem("pe_turns"), sem("pool_turns")

        def by_tile(a):
            return a.rearrange("(h p) d -> p h d", p=LO)

        with ExitStack() as part:
            def psb(name, shape, dt=F32):
                return sb("p_" + name, shape, dt, part)

            X = psb("X", [LO, HI, D])
            Y = psb("Y", [LO, HI, D])
            stat = psb("stat", [LO, 3, HI])
            heads_i = psb("heads_i", [1, ROWS], I32)
            heads_f = psb("heads_f", [1, ROWS])
            heads = psb("heads", [GROUPS, ROWS])
            ones = psb("ones", [1, P])
            limit_i = psb("limit_i", [GROUPS, NB], I32)
            limit = psb("limit", [GROUPS, NB])
            row_f = psb("row_f", [GROUPS, NB])
            row_i = psb("row_i", [GROUPS, NB], I32)
            begin_f = psb("begin_f", [GROUPS, NB])
            begin_i = psb("begin_i", [GROUPS, NB], I32)
            rows = psb("rows", [GROUPS, 4, ROW], I32)
            below = psb("below", [GROUPS, 512])
            ws = psb("ws", [GROUPS, NB, P], I32)
            wd = psb("wd", [GROUPS, NB, P], I32)
            hi_f = psb("hi_f", [GROUPS, NB, P])
            lo_f = ws[:, :, :].bitcast(F32)
            off = wd[:, :, :].bitcast(F32)
            ok = X[0:GROUPS, 0:HI // 2, :].rearrange("p h d -> p (h d)").rearrange("p (t e) -> p t e", t=NB)
            rel_i = psb("rel_i", [LO, NS, SR], I32)
            base_f = psb("base_f", [1, NS])
            Y2 = X[:, :, :].rearrange("p h d -> p (h d)")
            cnt = psb("cnt", [GROUPS, NB, G])
            hT_sb = psb("hT_sb", [D, 2, BLOCK])

            def ps(name):
                return sem("p_" + name, part)

            ld_x, ld_heads, ld_w = ps("ld_x"), ps("ld_heads"), ps("ld_w")
            heads_f_ok, heads_ps, row_ok, begin_ok, c_ok = ps("heads_f_ok"), ps("heads_ps"), ps("row_ok"), ps("begin_ok"), ps("c_ok")
            row_in = [pool_dma_sem(f"p_row_in{i}") for i in range(4)]
            row_used, limits_ok = ps("row_used"), ps("limits_ok")
            dst_in, src_in = pool_dma_sem("p_dst_in"), pool_dma_sem("p_src_in")
            idx_turned, idx_copied, dve_step, act_step = ps("idx_turned"), ps("idx_copied"), ps("dve_step"), ps("act_step")
            varied, rooted, normed, h_turned, h_copied = (
                ps("varied"), ps("rooted"), ps("normed"), ps("h_turned"), ps("h_copied"))
            h_stored = [ps("h_stored0"), ps("h_stored1")]
            squared, centred, cnt_ok, cnt_stored, pool_step, halved = (
                ps("squared"), ps("centred"), ps("cnt_ok"), ps("cnt_stored"), ps("pool_step"), ps("halved"))
            ld_rel, base_f_ok, base_ps = ps("ld_rel"), ps("base_f_ok"), ps("base_ps")
            block = part.enter_context(nc.Block())

            @block.sync
            def _(sp):
                sp.dma_start(heads_i[:, :], dst.rearrange("(o r c) -> o r c", o=1, c=ROW)[:, :, 0],
                             allow_slow_non_contiguous=True).then_inc(ld_heads, 16)
                sp.dma_start(X[:, :, :], by_tile(x)).then_inc(ld_x, 16)
                sp.dma_start(base_i[:, :], dst.rearrange("(o s c) -> o s c", o=1, c=LO * SR)[:, :, 0],
                             allow_slow_non_contiguous=True).then_inc(ld_rel, 16)
                sp.dma_start(rel_i[:, :, :], dst.rearrange("(s p r) -> p s r", p=LO, r=SR)).then_inc(ld_rel, 16)
                sp.dma_start(wl[0:D, :, :], Wl.rearrange("l i o -> i l o")).then_inc(ld_w, 16)
                sp.dma_start(wl[D:P, :, :], Wl.rearrange("l i o -> i l o")).then_inc(ld_w, 16)
                sp.dma_start(wr[0:D, :, :], Wr.rearrange("l i o -> i l o")).then_inc(ld_w, 16)
                sp.dma_start(wr[D:D + 1, :, :], b.unsqueeze(0)).then_inc(ld_w, 16)
                sp.dma_start(w0a[0:D, :], W0[0:D, :]).then_inc(ld_w, 16)
                sp.dma_start(w0a[D:P, :], W0[0:D, :]).then_inc(ld_w, 16)
                sp.dma_start(w0v[:, :], W0[D:2 * D, :]).then_inc(ld_w, 16)
                sp.dma_start(w1[:, :], W1).then_inc(ld_w, 16)
                sp.dma_start(w2[:, :], W2).then_inc(ld_w, 16)
                sp.dma_start(b01[:, 0:1], b0.unsqueeze(1)).then_inc(ld_w, 16)
                sp.dma_start(b01[:, 1:2], b1.unsqueeze(1)).then_inc(ld_w, 16)
                for k in range(SUBS):
                    sp.dma_start(b2_bc[:, k, :], b2.unsqueeze(0).broadcast_to((LO, D))).then_inc(ld_w, 16)
                for t in range(NB):
                    sp.wait_ge(h_copied, t + 1)
                    sp.dma_start(h_T[0][:, BLOCK * t:BLOCK * (t + 1)], hT_sb[:, t % 2, :]).then_inc(h_stored[t % 2], 16)
                sp.wait_ge(cnt_ok, 1)
                sp.dma_start(rcnt_d.rearrange("o (b g f) -> (o g) b f", g=GROUPS, f=G), cnt[:, :, :]).then_inc(cnt_stored, 16)
                sp.wait_ge(cnt_stored, 16)
                sp.wait_ge(h_stored[0], 16 * ((NB + 1) // 2))
                sp.wait_ge(h_stored[1], 16 * (NB // 2))
                sp.wait_ge(ld_w, 16 * 15)

            @block.gpsimd
            def _(pool):
                nc.gpsimd.memset(ones[:, :], 1.0).then_inc(constants, 1)
                nc.gpsimd.iota(limit_i[:, :], pattern=[[BLOCK, NB]], base=0, channel_multiplier=G).then_inc(limits_ok, 1)
                nc.gpsimd.memset(ident[:, :], 0.0).then_inc(pool_step, 1)
                nc.gpsimd.memset(flags[:, :], 0.0).then_inc(constants, 1)
                pool.wait_ge(pool_step, 1)
                nc.gpsimd.affine_select(out=ident[:, :], in_=ident[:, :], compare_op=ALU.not_equal, fill=1.0,
                                        base=0, pattern=[[-1, P]], channel_multiplier=1).then_inc(constants, 1)
                pool.wait_ge(row_ok, 1)
                for t in range(NB):
                    if t >= 4:
                        pool.wait_ge(row_used, t - 3)
                    nc.gpsimd.indirect_dma_start(
                        out=rows[:, t % 4, :], out_offset=None, in_=dst.rearrange("(r c) -> r c", c=ROW),
                        in_offset=bass.IndirectOffsetOnAxis(ap=row_i[:, t:t + 1], axis=0)).then_inc(row_in[t % 4], 16)
                pool.wait_ge(begin_ok, 1)
                for list_, to, win_in in ((dst, wd, dst_in), (src, ws, src_in)):
                    for t in range(NB):
                        nc.gpsimd.indirect_dma_start(
                            out=to[:, t, :], out_offset=None, in_=list_.unsqueeze(1),
                            in_offset=bass.IndirectOffsetOnAxis(ap=begin_i[:, t:t + 1], axis=0)).then_inc(win_in, 16)
                pool.wait_ge(dst_in, 16 * NB)
                pool.wait_ge(src_in, 16 * NB)

            @block.tensor
            def _(pe):
                pe.wait_ge(constants, 3)
                pe.wait_ge(heads_f_ok, 1)
                nc.tensor.matmul(ps_S[0][0:GROUPS, 0:ROWS], ones[:, 0:GROUPS], heads_f[:, :], start=True, stop=True).then_inc(heads_ps, 1)
                pe.wait_ge(base_f_ok, 1)
                nc.tensor.matmul(ps_mix[0:LO, 0:NS], ones[:, 0:LO], base_f[:, :], start=True, stop=True).then_inc(base_ps, 1)
                pe.wait_ge(normed, 1)
                for t in range(NB):
                    if t >= 2:
                        pe.wait_ge(h_copied, t - 1)
                    for k in range(SUBS):
                        last = nc.tensor.transpose(ps_build[t % 2][0:D, 0, LO * k:LO * (k + 1)], Y[:, SUBS * t + k, :], ident[0:LO, 0:LO])
                    last.then_inc(h_turned, 1)
                pe.wait_ge(c_ok, 1)
                for t in range(NB):
                    if t >= 2:
                        pe.wait_ge(idx_copied, t - 1)
                    nc.tensor.transpose(ps_S[t % 2][:, 0:GROUPS], lo_f[:, t, :], ident[0:GROUPS, 0:GROUPS])
                    nc.tensor.transpose(ps_S[t % 2][:, 256:256 + GROUPS], hi_f[:, t, :], ident[0:GROUPS, 0:GROUPS]).then_inc(idx_turned, 1)

            @block.scalar
            def _(act):
                act.wait_ge(centred, 1)
                nc.scalar.activation(X[:, :, :], Y[:, :, :], ACT.Square).then_inc(squared, 1)
                act.wait_ge(varied, 1)
                nc.scalar.activation(stat[:, 1, :], stat[:, 1, :], ACT.Sqrt).then_inc(rooted, 1)
                act.wait_ge(normed, 1)
                nc.scalar.activation(H[0][:, :, 0:D], Y[:, :, :], ACT.Copy).then_inc(act_step, 1)
                act.wait_ge(act_step, 1)
                nc.scalar.activation(X[:, :, :], H[0][:, :, 0:D], ACT.Copy, scale=LOW_SCALE).then_inc(halved, 1)
                for t in range(NB):
                    act.wait_ge(h_turned, t + 1)
                    if t >= 2:
                        act.wait_ge(h_stored[t % 2], 16 * (t // 2))
                    nc.scalar.copy(hT_sb[:, t % 2, :], ps_build[t % 2][0:D, 0, 0:BLOCK]).then_inc(h_copied, 1)
                for t in range(NB):
                    act.wait_ge(idx_turned, t + 1)
                    nc.scalar.copy(low[:, GROUPS * t:GROUPS * (t + 1)], ps_S[t % 2][:, 0:GROUPS])
                    nc.scalar.copy(col[:, GROUPS * t:GROUPS * (t + 1)], ps_S[t % 2][:, 256:256 + GROUPS]).then_inc(idx_copied, 1)

            @block.vector
            def _(dve):
                count = [0]

                def step(ins):
                    count[0] += 1
                    ins.then_inc(dve_step, 1)
                    dve.wait_ge(dve_step, count[0])

                dve.wait_ge(constants, 3)
                def norm():
                    m = stat[:, 0, :]
                    step(nc.vector.tensor_reduce(m, X[:, :, :], AX.X, ALU.add))
                    step(nc.vector.tensor_scalar(m, m, 1.0 / D, None, ALU.mult))
                    nc.vector.tensor_tensor(Y[:, :, :], X[:, :, :], m.unsqueeze(2).broadcast_to((LO, HI, D)),
                                            ALU.subtract).then_inc(centred, 1)

                dve.wait_ge(ld_heads, 16)
                nc.vector.tensor_copy(heads_f[:, :], heads_i[:, :]).then_inc(heads_f_ok, 1)
                dve.wait_ge(limits_ok, 1)
                step(nc.vector.tensor_copy(limit[:, :], limit_i[:, :]))
                dve.wait_ge(heads_ps, 1)
                step(nc.vector.tensor_copy(heads[:, :], ps_S[0][0:GROUPS, 0:ROWS]))
                for t in range(NB):
                    step(nc.vector.tensor_scalar(below[:, 0:ROWS], heads[:, :], limit[:, t:t + 1], 0.0, ALU.is_lt, ALU.add,
                                                 accum_out=row_f[:, t:t + 1]))
                step(nc.vector.tensor_scalar(row_f[:, :], row_f[:, :], -1.0, 0.0, ALU.add, ALU.max))
                nc.vector.tensor_copy(row_i[:, :], row_f[:, :]).then_inc(row_ok, 1)
                for t in range(NB):
                    dve.wait_ge(row_in[t % 4], 16 * (t // 4 + 1))
                    step(nc.vector.tensor_copy(below[:, 0:ROW], rows[:, t % 4, :]))
                    step(nc.vector.tensor_scalar(below[:, 0:ROW], below[:, 0:ROW], limit[:, t:t + 1], 0.0, ALU.is_lt, ALU.add,
                                                 accum_out=begin_f[:, t:t + 1]))
                    dve.sem_inc(row_used, 1)
                step(nc.vector.scalar_tensor_tensor(begin_f[:, :], row_f[:, :], float(ROW), begin_f[:, :], ALU.mult, ALU.add))
                step(nc.vector.tensor_scalar(begin_f[:, :], begin_f[:, :], float(E - P), None, ALU.min))
                nc.vector.tensor_copy(begin_i[:, :], begin_f[:, :]).then_inc(begin_ok, 1)
                dve.wait_ge(ld_x, 16)
                norm()
                dve.wait_ge(ld_rel, 32)
                nc.vector.tensor_copy(base_f[:, :], base_i[:, :]).then_inc(base_f_ok, 1)
                dve.wait_ge(squared, 1)
                v = stat[:, 1, :]
                step(nc.vector.tensor_reduce(v, X[:, :, :], AX.X, ALU.add))
                nc.vector.tensor_scalar(v, v, 1.0 / D, EPS, ALU.mult, ALU.add).then_inc(varied, 1)
                dve.wait_ge(rooted, 1)
                step(nc.vector.reciprocal(v, v))
                step(nc.vector.tensor_tensor(Y[:, :, :], Y[:, :, :], v.unsqueeze(2).broadcast_to((LO, HI, D)), ALU.mult))
                nc.vector.tensor_scalar(Y[:, :, :], Y[:, :, :], 0.0, None, ALU.max).then_inc(normed, 1)
                dve.wait_ge(halved, 1)
                step(nc.vector.scalar_tensor_tensor(H[0][:, :, D:2 * D], Y[:, :, :], LOW_SCALE, X[:, :, :], ALU.mult, ALU.subtract))
                dve.wait_ge(ld_w, 16 * 15)
                step(nc.vector.tensor_scalar(wl[D:P, :, :], wl[D:P, :, :], 1.0 / LOW_SCALE, None, ALU.mult))
                step(nc.vector.tensor_scalar(w0a[D:P, :], w0a[D:P, :], 1.0 / LOW_SCALE, None, ALU.mult))
                rel_f = Y2[:, NS * SR:2 * NS * SR]
                rel3 = rel_f.rearrange("p (s r) -> p s r", r=SR)
                step(nc.vector.tensor_copy(rel3, rel_i[:, :, :]))
                dve.wait_ge(base_ps, 1)
                step(nc.vector.tensor_tensor(rel3, rel3, ps_mix[0:LO, 0:NS].unsqueeze(2).broadcast_to((LO, NS, SR)), ALU.subtract))
                in_span = Y2[:, 0:NS * SR]
                nc.vector.tensor_copy(rel[:, :], rel_f)
                step(nc.vector.tensor_scalar(in_span, rel_f, 0.0, None, ALU.is_ge))
                step(nc.vector.scalar_tensor_tensor(in_span, rel_f, SPAN - 0.5, in_span, ALU.is_lt, ALU.mult))
                step(nc.vector.tensor_reduce(flags[0:LO, 1:2], in_span, AX.X, ALU.add))
                dve.wait_ge(dst_in, 16 * NB)
                step(nc.vector.tensor_copy(off[:, :, :], wd[:, :, :]))
                step(nc.vector.tensor_tensor(off[:, :, :], off[:, :, :], limit[:, :].unsqueeze(2).broadcast_to((GROUPS, NB, P)), ALU.subtract))
                step(nc.vector.tensor_scalar(ok[:, :, :], off[:, :, :], 0.0, None, ALU.is_ge))
                step(nc.vector.scalar_tensor_tensor(ok[:, :, :], off[:, :, :], G - 0.5, ok[:, :, :], ALU.is_lt, ALU.mult))
                dve.wait_ge(src_in, 16 * NB)
                magic = 1.5 * 2.0 ** 23
                step(nc.vector.tensor_copy(lo_f[:, :, :], ws[:, :, :]))
                step(nc.vector.tensor_scalar(hi_f[:, :, :], lo_f[:, :, :], -float(LO // 2), 1.0 / LO, ALU.add, ALU.mult))
                step(nc.vector.tensor_scalar(hi_f[:, :, :], hi_f[:, :, :], magic, None, ALU.add))
                step(nc.vector.tensor_scalar(hi_f[:, :, :], hi_f[:, :, :], magic, None, ALU.subtract))
                step(nc.vector.scalar_tensor_tensor(lo_f[:, :, :], hi_f[:, :, :], -float(LO), lo_f[:, :, :], ALU.mult, ALU.add))
                step(nc.vector.scalar_tensor_tensor(hi_f[:, :, :], hi_f[:, :, :], float(G), off[:, :, :], ALU.mult, ALU.add))
                step(nc.vector.scalar_tensor_tensor(hi_f[:, :, :], hi_f[:, :, :], 1.0, ok[:, :, :], ALU.add, ALU.mult))
                nc.vector.tensor_scalar(hi_f[:, :, :], hi_f[:, :, :], -1.0, None, ALU.add).then_inc(c_ok, 1)
                for f in range(G):
                    step(nc.vector.tensor_scalar(ok[:, :, :], off[:, :, :], float(f), None, ALU.is_equal))
                    step(nc.vector.tensor_reduce(cnt[:, :, f], ok[:, :, :], AX.X, ALU.add))
                step(nc.vector.tensor_reduce(flags[0:GROUPS, 0:1], cnt[:, :, :], AX.XY, ALU.add))
                step(nc.vector.tensor_scalar(cnt[:, :, :], cnt[:, :, :], 1.0, None, ALU.max))
                nc.vector.reciprocal(cnt[:, :, :], cnt[:, :, :]).then_inc(cnt_ok, 1)

        A0 = sb("A0", [P, (HI + 1) * BLOCK], F8)
        A1S = sb("A1S", [P, N + SPAN])
        A1 = A1S[:, 0:(HI + 1) * BLOCK // 4].bitcast(F8)
        rcb = sb("rcb", [P, BLOCK])
        hT_in = sb("hT_in", [D + 1, BLOCK])
        h_rows = sb("h_rows", [LO, SUBS, D])
        hT_out = sb("hT_out", [D, BLOCK])
        scaled = [sb(f"scaled{i}", [P, BLOCK]) for i in range(2)]
        halves = sb("halves", [LO, SUBS, 2 * D], F16)
        big = sb("big", [LO, SUBS, D])
        top = sb("top", [LO, 2])

        chunk_in = [[sem(f"chunk_in{l}_{c}") for c in range(CHUNKS)] for l in range(1, LAYERS)]

        def load_chunk(sp, l, t, c):
            at = slice(c * CHUNK * BLOCK, (c + 1) * CHUNK * BLOCK)
            sp.dma_start(A0[:, at].bitcast(U8), matrix[bass.ds(t, 1), :, at].rearrange("o p c -> (o p) c")).then_inc(chunk_in[l - 1][c], 16)

        def hold(eng, turns, sem_, value, *more):
            eng.wait_ge(sem_, value)
            for s_, v_ in more:
                eng.wait_ge(s_, v_)
            eng.sem_inc(turns, 1)

        class Node:
            def __init__(self, layer, stack):
                def s(name):
                    return sem(f"{name}{layer}", stack)
                self.summed = [s("summed_a"), s("summed_b")]
                self.scaled = [s("scaled_a"), s("scaled_b")]
                by = s if layer == 0 else lambda name: pool_dma_sem(f"{name}{layer}")
                self.in_ = by("node_in")
                self.hT_in = by("hT_in")
                self.mixed = s("mixed")
                if layer < LAYERS - 1:
                    self.stored = by("stored")
                    self.acted, self.turned, self.high, self.big, self.low, self.placed = (
                        s("acted"), s("turned"), s("high"), s("big"), s("low"), s("placed"))
                    self.step, self.free, self.copied = s("node_step"), s("free"), s("copied")

        def node_pe_mix(pe, nd, l, j):
            hold(pe, pe_turns, nd.scaled[0], j + 1, (nd.scaled[1], j + 1), (nd.hT_in, 16 * j + 16))
            for k in range(SUBS):
                to, at = ps_mix[0:LO, D * k:D * (k + 1)], slice(LO * k, LO * (k + 1))
                nc.tensor.matmul(to, scaled[0][:, at], wl[:, l, :], start=True, stop=False)
                nc.tensor.matmul(to, scaled[1][:, at], wl[:, l, :], start=False, stop=False)
                last = nc.tensor.matmul(to, hT_in[:, at], wr[:, l, :], start=False, stop=True)
            last.then_inc(nd.mixed, 1)

        def node_pe_turn(pe, nd, j):
            hold(pe, pe_turns, nd.acted, j + 1)
            for k in range(SUBS):
                last = nc.tensor.transpose(ps_turn[0:D, LO * k:LO * (k + 1)], h_rows[:, k, :], ident[0:LO, 0:LO])
            last.then_inc(nd.turned, 1)

        def node_dve_scale(dve, nd, half, j):
            dve.wait_ge(nd.in_, 16 * j + 16)
            dve.wait_ge(nd.summed[half], j + 1)
            nc.vector.tensor_tensor(scaled[half][:, :], ps_S[half][:, 0:BLOCK], rcb[:, :], ALU.mult).then_inc(nd.scaled[half], 1)

        def node_dve_low(dve, nd, j):
            dve.wait_ge(nd.acted, j + 1)
            dve.wait_ge(nd.big, j + 1)
            nc.vector.scalar_tensor_tensor(halves[:, :, D:2 * D], h_rows[:, :, :], LOW_SCALE, big[:, :, :],
                                           ALU.mult, ALU.subtract).then_inc(nd.step, 1)
            nc.vector.tensor_reduce(top[:, 0:1], h_rows[:, :, :], AX.XY, ALU.max).then_inc(nd.step, 1)
            dve.wait_ge(nd.step, 2 * j + 2)
            nc.vector.tensor_tensor(flags[0:LO, 3:4], flags[0:LO, 3:4], top[:, 0:1], ALU.max).then_inc(nd.low, 1)

        def node_act_relu(act, nd, j):
            mixed = ps_mix[0:LO, 0:SUBS * D].rearrange("p (k d) -> p k d", d=D)
            act.wait_ge(nd.mixed, j + 1)
            act.wait_ge(nd.placed, j + 1)
            nc.scalar.activation(halves[:, :, 0:D], mixed, ACT.Relu).then_inc(nd.high, 1)
            nc.scalar.activation(h_rows[:, :, :], mixed, ACT.Relu).then_inc(nd.acted, 1)

        def node_act_turn(act, nd, j):
            act.wait_ge(nd.turned, j + 1)
            act.wait_ge(nd.free, j + 1)
            nc.scalar.copy(hT_out[:, :], ps_turn[0:D, 0:BLOCK]).then_inc(nd.copied, 1)

        def node_pool(pool, nd, l, j):
            hold(pool, pool_turns, nd.high, j + 1)
            nc.gpsimd.tensor_scalar(big[:, :, :], halves[:, :, 0:D], LOW_SCALE, None, ALU.mult).then_inc(nd.big, 1)
            hold(pool, pool_turns, nd.low, j + 1)
            nc.gpsimd.tensor_copy(H[(l + 1) % 2][:, bass.ds(SUBS * j, SUBS), :], halves[:, :, :]).then_inc(nd.placed, 1)

        def node_sp_load(sp, nd, l, j, first=False):
            if not first:
                hold(sp, sp_turns, nd.scaled[0], j, (nd.scaled[1], j), (nd.mixed, j))
            sp.dma_start(rcb[:, :], rcnt_d[0:1, bass.ds(BLOCK * j, BLOCK)].broadcast_to((P, BLOCK))).then_inc(nd.in_, 16)
            sp.dma_start(hT_in[0:D, :], h_T[l][:, bass.ds(BLOCK * j, BLOCK)]).then_inc(nd.hT_in, 16)

        def node_sp_store(sp, nd, l, j):
            hold(sp, sp_turns, nd.copied, j + 1)
            sp.dma_start(h_T[l + 1][:, bass.ds(BLOCK * j, BLOCK)], hT_out[:, :]).then_inc(nd.stored, 16)
            hold(sp, nd.free, nd.stored, 16 * j + 16)

        with ExitStack() as part:
            iota_c = sb("iota_c", [P, 512], F16, part)
            onehot_c = sb("onehot_c", [P, OH_SLOTS, PAIR, COLS], F16, part)
            onehot_l = sb("onehot_l", [P, OH_SLOTS, PAIR, P], F16, part)
            rowmax = sb("rowmax", [P, NB], F32, part)
            colx = sb("colx", [P, 2, GROUPS], F32, part)

            def bs(name):
                return sem("b_" + name, part)

            iota_ok, onehots, built, evacuated, agged, rows_ok = (
                bs("iota_ok"), bs("onehots"), bs("built"), bs("evacuated"), bs("agged"), bs("rows_ok"))
            a_stored = [bs("a_stored0"), bs("a_stored1")]
            colx_ok, pool_onehots = bs("colx_ok"), bs("pool_onehots")
            nd = Node(0, part)
            A = [A0[:, :], A1]
            countrow = [a[:, HI * BLOCK:(HI + 1) * BLOCK].bitcast(U8) for a in A]
            block = part.enter_context(nc.Block())

            def turns(eng, body):
                body(0, 0)
                body(1, 1)
                with eng.Fori(1, (NB - 1) // 2) as m:
                    body(m * 2, 0)
                    body(m * 2 + 1, 1)
                for i in range(NB - 1, NB + 2):
                    body(i, i % 2)

            def does(i, lag):
                return 0 <= i - lag < NB if isinstance(i, int) else True

            @block.sync
            def _(sp):
                def body(i, par):
                    if does(i, 1):
                        hold(sp, sp_turns, evacuated, i * UNITS)
                        for c in range(CHUNKS):
                            at = slice(c * CHUNK * BLOCK, (c + 1) * CHUNK * BLOCK)
                            sp.dma_start(matrix[bass.ds(i - 1, 1), :, at].rearrange("o p c -> (o p) c"),
                                         A[1 - par][:, at].bitcast(U8)).then_inc(a_stored[1 - par], 16)
                        node_sp_load(sp, nd, 0, i - 1, first=isinstance(i, int) and i == 1)
                    if does(i, 2):
                        node_sp_store(sp, nd, 0, i - 2)
                turns(sp, body)
                sp.wait_ge(a_stored[0], 16 * CHUNKS * ((NB + 1) // 2))
                sp.wait_ge(a_stored[1], 16 * CHUNKS * (NB // 2))
                sp.wait_ge(nd.summed[1], NB)
                sp.wait_ge(rows_ok, NB)
                for c in range(CHUNKS):
                    load_chunk(sp, 1, 0, c)
                sp.wait_ge(nd.stored, 16 * NB)

            @block.gpsimd
            def _(pool):
                nc.gpsimd.iota(iota_c[:, :], pattern=[[1, 512]], base=0, channel_multiplier=0,
                               allow_small_or_imprecise_dtypes=True).then_inc(iota_ok, 1)
                nc.gpsimd.memset(onehot_c[:, :, :, BLOCK:BLOCK + 1], 1.0).then_inc(iota_ok, 1)
                nc.gpsimd.memset(onehot_c[:, :, :, BLOCK + 1:COLS], 0.0).then_inc(iota_ok, 1)
                pool.sem_inc(nd.free, 1)
                pool.sem_inc(nd.placed, 1)

                def body(i, par):
                    for k in range(UNITS):
                        if does(i, 0) and k % OH_SLOTS == POOL_SLOT:
                            more = [(built, i * UNITS + k + 1 - OH_SLOTS)] if not (isinstance(i, int) and i == 0 and k < OH_SLOTS) else []
                            hold(pool, pool_turns, colx_ok, i + 1, *more)
                            for g in range(PAIR):
                                at = PAIR * k + g
                                last = nc.gpsimd.tensor_scalar(onehot_l[:, POOL_SLOT, g, :], iota_c[:, 0:P], colx[:, 1, at:at + 1],
                                                               None, ALU.is_equal)
                            last.then_inc(pool_onehots, 1)
                        if does(i, 2) and k == 28:
                            node_pool(pool, nd, 0, i - 2)
                turns(pool, body)

            @block.tensor
            def _(pe):
                pe.wait_ge(iota_ok, 4)

                def body(i, par):
                    for k in range(UNITS):
                        if does(i, 0):
                            slot = k % OH_SLOTS
                            pe.wait_ge(onehots, i * UNITS + k + 1)
                            if slot == POOL_SLOT:
                                pe.wait_ge(pool_onehots, i * (UNITS // OH_SLOTS) + k // OH_SLOTS + 1)
                            if not (isinstance(i, int) and i == 0 and k < PS_SLOTS):
                                pe.wait_ge(evacuated, i * UNITS + k + 1 - PS_SLOTS)
                            for g in range(PAIR):
                                last = nc.tensor.matmul(ps_build[k % PS_SLOTS][:, g, 0:COLS], onehot_l[:, slot, g, :],
                                                        onehot_c[:, slot, g, :], start=True, stop=True)
                            last.then_inc(built, 1)
                        if does(i, 1):
                            if k == 0:
                                more = [(nd.scaled[0], i - 1)] if not (isinstance(i, int) and i == 1) else []
                                hold(pe, pe_turns, evacuated, i * UNITS, *more)
                            if k == UNITS // 2 and not (isinstance(i, int) and i == 1):
                                hold(pe, pe_turns, nd.scaled[1], i - 1)
                            half = k // (UNITS // 2)
                            for q in range(2):
                                h = 2 * k + q
                                last = nc.tensor.matmul(ps_S[half][:, 0:BLOCK], H[0][:, h, :], A[1 - par][0:LO, h * BLOCK:(h + 1) * BLOCK],
                                                        start=h % (HI // 2) == 0, stop=h % (HI // 2) == HI // 2 - 1)
                            if k % (UNITS // 2) == UNITS // 2 - 1:
                                last.then_inc(nd.summed[half], 1)
                        if does(i, 2) and k == 8:
                            node_pe_mix(pe, nd, 0, i - 2)
                        if does(i, 2) and k == 18:
                            node_pe_turn(pe, nd, i - 2)
                turns(pe, body)

            @block.scalar
            def _(act):
                def body(i, par):
                    for k in range(UNITS):
                        if does(i, 0):
                            more = []
                            if k == 0 and not (isinstance(i, int) and i < 2):
                                more = [(nd.summed[1], i - 1)]
                                more.append((rows_ok, i - 1))
                                more.append((a_stored[par], (i - par) * (8 * CHUNKS)))
                            hold(act, act_turns, built, i * UNITS + k + 1, *more)
                            to = A[par].rearrange("p (h g f) -> p g h f", h=HI + 1, f=G)[:, PAIR * k:PAIR * (k + 1), :, :]
                            nc.scalar.activation(to, ps_build[k % PS_SLOTS][:, :, 0:COLS].rearrange("p g (h f) -> p g h f", f=G),
                                                 ACT.Copy, saturate=True).then_inc(evacuated, 1)
                        if does(i, 2) and k == 10:
                            node_act_relu(act, nd, i - 2)
                        if does(i, 2) and k == 22:
                            node_act_turn(act, nd, i - 2)
                turns(act, body)

            @block.vector
            def _(dve):
                nc.vector.memset(hT_in[D:D + 1, :], 1.0).then_inc(iota_ok, 1)
                dve.wait_ge(iota_ok, 4)

                def body(i, par):
                    if does(i, 0):
                        if not (isinstance(i, int) and i == 0):
                            dve.wait_ge(built, i * UNITS)
                        nc.vector.tensor_copy(colx[:, 0, :], col[:, bass.ds(i * GROUPS, GROUPS)])
                        nc.vector.tensor_copy(colx[:, 1, :], low[:, bass.ds(i * GROUPS, GROUPS)]).then_inc(colx_ok, 1)
                        dve.wait_ge(colx_ok, i + 1)
                    for k in range(UNITS):
                        if does(i, 0):
                            slot = k % OH_SLOTS
                            if not (isinstance(i, int) and i == 0 and k < OH_SLOTS):
                                dve.wait_ge(built, i * UNITS + k + 1 - OH_SLOTS)
                            for g in range(PAIR):
                                at = PAIR * k + g
                                last = nc.vector.tensor_scalar(onehot_c[:, slot, g, 0:BLOCK], iota_c[:, 0:BLOCK], colx[:, 0, at:at + 1], None, ALU.is_equal)
                                if slot != POOL_SLOT:
                                    last = nc.vector.tensor_scalar(onehot_l[:, slot, g, :], iota_c[:, 0:P], colx[:, 1, at:at + 1], None, ALU.is_equal)
                            last.then_inc(onehots, 1)
                        if does(i, 1) and k == UNITS // 2 + 4:
                            node_dve_scale(dve, nd, 0, i - 1)
                        if does(i, 1) and k == 2:
                            dve.wait_ge(evacuated, i * UNITS)
                            nc.vector.tensor_reduce(rowmax[:, bass.ds(i - 1, 1)], countrow[1 - par], AX.X, ALU.max).then_inc(rows_ok, 1)
                        if does(i, 2) and k == 3:
                            node_dve_scale(dve, nd, 1, i - 2)
                        if does(i, 2) and k == 26:
                            node_dve_low(dve, nd, i - 2)
                turns(dve, body)
                dve.wait_ge(rows_ok, NB)
                nc.vector.tensor_reduce(flags[:, 2:3], rowmax[:, :], AX.X, ALU.max).then_inc(rows_ok, 1)

        def layer(l):
            last_layer = l == LAYERS - 1
            with ExitStack() as part:
                def ls(name):
                    return sem(f"l{l}_{name}", part)

                def lsb(name, shape, dt=F32):
                    return sb(f"l{l}_{name}", shape, dt, part)

                loaded = chunk_in[l - 1]
                nd = Node(l, part)
                consumed = [ls(f"consumed{c}") for c in range(CHUNKS - 1)] + [nd.summed[1]]
                if last_layer:
                    x_in = lsb("x_in", [LO, SUBS, D])
                    x1 = lsb("x1", [LO, SUBS, D])
                    xc = lsb("xc", [LO, SUBS, D])
                    sq = lsb("sq", [LO, SUBS, D])
                    agg = lsb("agg", [P, BLOCK])
                    x1b = lsb("x1b", [LO, SUBS, D])
                    result = lsb("result", [LO, SUBS, D])
                    st = lsb("st", [LO, 3, SUBS])
                    h2T = lsb("h2T", [D, BLOCK])
                    y0 = lsb("y0", [D, BLOCK])
                    y1 = lsb("y1", [D, BLOCK])
                    x_ok, aggd, x1_ok, centred, squared, varied, rooted, normed, turned2, h2_ok = (
                        pool_dma_sem("l2_x_ok"), ls("aggd"), ls("x1_ok"), ls("centred"), ls("squared"), ls("varied"), ls("rooted"),
                        ls("normed"), ls("turned2"), ls("h2_ok"))
                    p0, y0_ok, p1, y1_ok, p2, x1b_ok, out_ok, out_stored, out_free, step = (
                        ls("p0"), ls("y0_ok"), ls("p1"), ls("y1_ok"), ls("p2"), ls("x1b_ok"), ls("out_ok"),
                        pool_dma_sem("l2_out_stored"), ls("out_free"), ls("step"))
                else:
                    iota_s = lsb("iota_s", [P, SPAN], F16)
                    edges = lsb("edges", [LO, 2, SR, D])
                    edge_halves = lsb("edge_halves", [LO, 2, SR, 2 * D], F16)
                    onehot = lsb("onehot", [LO, 2, SR, SPAN], F16)
                    relx = lsb("relx", [LO, 2, SR])
                    emax = lsb("emax", [LO, NS])
                    edges_in = [ls("edges_in0"), ls("edges_in1")]
                    hot, esummed, eadded, relx_ok, zeroed = ls("hot"), ls("esummed"), ls("eadded"), ls("relx_ok"), ls("zeroed")
                    ehigh, eresid, esplit, emaxed = ls("ehigh"), ls("eresid"), ls("esplit"), ls("emaxed")
                SE = A1S[:, :]
                node_rows = "(b k p) d -> b p k d"
                block = part.enter_context(nc.Block())

                def turns(eng, body):
                    body(0)
                    with eng.Fori(1, NB - 1) as b_:
                        body(b_)
                    body(NB - 1)
                    body(NB)

                def multiplies(t):
                    return not (isinstance(t, int) and t == NB)

                def is_last(t):
                    return isinstance(t, int) and t == NB - 1

                def has_node(t):
                    return not (isinstance(t, int) and t == 0)

                @block.sync
                def _(sp):
                    with sp.Fori(1, NB) as t:
                        for c in range(CHUNKS):
                            hold(sp, sp_turns, consumed[c], t)
                            load_chunk(sp, l, t, c)
                    if not last_layer:
                        for c in range(CHUNKS):
                            sp.wait_ge(consumed[c], NB)
                            load_chunk(sp, l + 1, 0, c)

                @block.gpsimd
                def _(pool):
                    if not last_layer:
                        nc.gpsimd.memset(A1S[:, :], 0.0).then_inc(zeroed, 1)
                        nc.gpsimd.iota(iota_s[:, :], pattern=[[1, SPAN]], base=0, channel_multiplier=0,
                                       allow_small_or_imprecise_dtypes=True).then_inc(zeroed, 1)
                        pool.sem_inc(nd.free, 1)
                        pool.sem_inc(nd.placed, 1)
                    else:
                        pool.sem_inc(out_free, 1)

                    def body(t):
                        if multiplies(t):
                            if has_node(t):
                                more = [(aggd, t)] if last_layer else []
                                hold(pool, pool_turns, nd.scaled[0], t, (nd.scaled[1], t), (nd.mixed, t), *more)
                            pool.dma_start(rcb[:, :], rcnt_d[0:1, bass.ds(t * BLOCK, BLOCK)].broadcast_to((P, BLOCK))).then_inc(nd.in_, 16)
                            pool.dma_start(hT_in[0:D, :], h_T[l][:, bass.ds(t * BLOCK, BLOCK)]).then_inc(nd.hT_in, 16)
                            if last_layer:
                                if has_node(t):
                                    hold(pool, pool_turns, x1_ok, t)
                                pool.dma_start(x_in[:, :, :], x.rearrange(node_rows, k=SUBS, p=LO)[bass.ds(t, 1), :, :, :]
                                               .rearrange("o p k d -> (o p) k d")).then_inc(x_ok, 16)
                        if has_node(t) and not last_layer:
                            node_pool(pool, nd, l, t - 1)
                            hold(pool, pool_turns, nd.copied, t)
                            pool.dma_start(h_T[l + 1][:, bass.ds((t - 1) * BLOCK, BLOCK)], hT_out[:, :]).then_inc(nd.stored, 16)
                            hold(pool, nd.free, nd.stored, t * 16)
                        if has_node(t) and last_layer:
                            hold(pool, pool_turns, x1_ok, t)
                            nc.gpsimd.tensor_tensor(x1b[:, :, :], x1[:, :, :], b2_bc[:, :, :], ALU.add).then_inc(x1b_ok, 1)
                            hold(pool, pool_turns, out_ok, t)
                            pool.dma_start(out.rearrange(node_rows, k=SUBS, p=LO)[bass.ds(t - 1, 1), :, :, :]
                                           .rearrange("o p k d -> (o p) k d"), result[:, :, :]).then_inc(out_stored, 16)
                            hold(pool, out_free, out_stored, t * 16)
                    turns(pool, body)
                    if last_layer:
                        pool.wait_ge(out_stored, 16 * NB)
                    else:
                        pool.wait_ge(nd.stored, 16 * NB)

                def superchunk(pe, t, k):
                    slot = k % 2
                    waits = [(esplit, t * SC + k + 1)]
                    if not (isinstance(t, int) and t == 0 and k < 2):
                        waits.append((eadded, t * SC + k - 1))
                    hold(pe, pe_turns, hot, t * SC + k + 1, *waits)
                    for r in range(SR):
                        last = nc.tensor.matmul(ps_build[slot][:, 0, 0:SPAN], edge_halves[:, slot, r, :], onehot[:, slot, r, :],
                                                start=r == 0, stop=r == SR - 1)
                    last.then_inc(esummed, 1)

                @block.tensor
                def _(pe):
                    def body(t):
                        for h in range(HI):
                            half, c = h // (HI // 2), h // CHUNK
                            if multiplies(t):
                                if h % (HI // 2) == 0 and has_node(t):
                                    hold(pe, pe_turns, nd.scaled[half], t)
                                if h % CHUNK == 0:
                                    hold(pe, pe_turns, loaded[c], t * 16 + 16)
                                last = nc.tensor.matmul(ps_S[half][:, 0:BLOCK], H[l % 2][:, h, :], A0[0:LO, h * BLOCK:(h + 1) * BLOCK],
                                                        start=h % (HI // 2) == 0, stop=h % (HI // 2) == HI // 2 - 1)
                                if h % CHUNK == CHUNK - 1 and h < HI - 1:
                                    last.then_inc(consumed[c], 1)
                                if h % (HI // 2) == HI // 2 - 1:
                                    last.then_inc(nd.summed[half], 1)
                                if not last_layer and h % 25 == 20:
                                    superchunk(pe, t, h // 25)
                            if not has_node(t):
                                continue
                            j = t - 1
                            if h == (10 if last_layer else 32):
                                node_pe_mix(pe, nd, l, j)
                            if h == 62 and not last_layer:
                                node_pe_turn(pe, nd, j)
                            if last_layer:
                                if h == 44:
                                    hold(pe, pe_turns, normed, t)
                                    for k in range(SUBS):
                                        last2 = nc.tensor.transpose(ps_turn[0:D, LO * k:LO * (k + 1)], xc[:, k, :], ident[0:LO, 0:LO])
                                    last2.then_inc(turned2, 1)
                                if h == 52:
                                    hold(pe, pe_turns, h2_ok, t, (aggd, t))
                                    nc.tensor.matmul(ps_build[0][0:D, 0, 0:BLOCK], w0a[:, :], agg[:, :], start=True, stop=False)
                                    nc.tensor.matmul(ps_build[0][0:D, 0, 0:BLOCK], w0v[:, :], h2T[:, :], start=False, stop=True).then_inc(p0, 1)
                                if h == 64:
                                    hold(pe, pe_turns, y0_ok, t)
                                    nc.tensor.matmul(ps_build[0][0:D, 1, 0:BLOCK], w1[:, :], y0[:, :], start=True, stop=True).then_inc(p1, 1)
                                if h == 76:
                                    hold(pe, pe_turns, y1_ok, t)
                                    for k in range(SUBS):
                                        last2 = nc.tensor.matmul(ps_build[1][0:LO, 0, D * k:D * (k + 1)], y1[:, LO * k:LO * (k + 1)], w2[:, :],
                                                                 start=True, stop=True)
                                    last2.then_inc(p2, 1)
                    turns(pe, body)

                @block.scalar
                def _(act):
                    def fetch(t, k):
                        rows_ = attr.rearrange("(s p r) d -> s p r d", p=LO, r=SR)[bass.ds(t * SC + k, 1), :, :, :].rearrange("o p r d -> (o p) r d")
                        act.dma_start(edges[0:DMA_P, k % 2, :, :], rows_[0:DMA_P, :, :]).then_inc(edges_in[k % 2], 16)
                        act.dma_start(edges[DMA_P:LO, k % 2, :, :], rows_[DMA_P:LO, :, :]).then_inc(edges_in[k % 2], 16)

                    def body(t):
                        if multiplies(t) and not last_layer:
                            if not has_node(t):
                                fetch(t, 0)
                                fetch(t, 1)
                            for k in range(SC):
                                slot = k % 2
                                act.wait_ge(edges_in[slot], (t * (SC // 2) + k // 2 + 1) * 32)
                                if not (isinstance(t, int) and t == 0 and k < 2):
                                    act.wait_ge(esummed, t * SC + k - 1)
                                nc.scalar.activation(edge_halves[:, slot, :, 0:D], edges[:, slot, :, :], ACT.Copy).then_inc(ehigh, 1)
                                act.wait_ge(eresid, t * SC + k + 1)
                                nc.scalar.activation(edge_halves[:, slot, :, D:2 * D], edges[:, slot, :, :], ACT.Copy,
                                                     scale=LOW_SCALE).then_inc(esplit, 1)
                                act.wait_ge(esplit, t * SC + k + 1)
                                if k < 2:
                                    fetch(t, k + 2)
                                elif not is_last(t):
                                    fetch(t + 1, k - 2)
                                if has_node(t):
                                    if k == 1:
                                        node_act_relu(act, nd, t - 1)
                                    if k == 2:
                                        node_act_turn(act, nd, t - 1)
                        elif not last_layer:
                            node_act_relu(act, nd, t - 1)
                            node_act_turn(act, nd, t - 1)
                        if has_node(t) and last_layer:
                            act.wait_ge(centred, t)
                            nc.scalar.activation(sq[:, :, :], xc[:, :, :], ACT.Square).then_inc(squared, 1)
                            act.wait_ge(varied, t)
                            nc.scalar.activation(st[:, 1, :], st[:, 1, :], ACT.Sqrt).then_inc(rooted, 1)
                            act.wait_ge(turned2, t)
                            nc.scalar.activation(h2T[:, :], ps_turn[0:D, 0:BLOCK], ACT.Relu).then_inc(h2_ok, 1)
                            act.wait_ge(p0, t)
                            nc.scalar.activation(y0[:, :], ps_build[0][0:D, 0, 0:BLOCK], ACT.Relu, bias=b01[:, 0:1]).then_inc(y0_ok, 1)
                            act.wait_ge(p1, t)
                            nc.scalar.activation(y1[:, :], ps_build[0][0:D, 1, 0:BLOCK], ACT.Relu,
                                                 bias=b01[:, 1:2]).then_inc(y1_ok, 1)
                    turns(act, body)

                @block.vector
                def _(dve):
                    def hots(t, k):
                        slot = k % 2
                        dve.wait_ge(edges_in[slot], (t * (SC // 2) + k // 2 + 1) * 32)
                        nc.vector.tensor_reduce(emax[:, bass.ds(t * SC + k, 1)], edges[:, slot, :, :], AX.XY, ALU.max,
                                                apply_absolute_value=True).then_inc(emaxed, 1)
                        dve.wait_ge(emaxed, t * SC + k + 1)
                        dve.wait_ge(ehigh, t * SC + k + 1)
                        nc.vector.tensor_tensor(edges[:, slot, :, :], edges[:, slot, :, :], edge_halves[:, slot, :, 0:D],
                                                ALU.subtract).then_inc(eresid, 1)
                        if not (isinstance(t, int) and t == 0 and k < 2):
                            dve.wait_ge(esummed, t * SC + k - 1)
                        nc.vector.tensor_copy(relx[:, slot, :], rel[:, bass.ds(t * (SC * SR) + k * SR, SR)]).then_inc(relx_ok, 1)
                        dve.wait_ge(relx_ok, t * SC + k + 1)
                        for r in range(SR):
                            last = nc.vector.tensor_scalar(onehot[:, slot, r, :], iota_s[0:LO, :], relx[:, slot, r:r + 1], None, ALU.is_equal)
                        last.then_inc(hot, 1)

                    def add(t, k):
                        base = dve.value_load(base_i[0:1, bass.ds(t * SC + k, 1)], min_val=0, max_val=N - 1)
                        at = SE[:, bass.ds(base, SPAN)]
                        dve.wait_ge(esummed, t * SC + k + 1)
                        nc.vector.tensor_tensor(at, at, ps_build[k % 2][:, 0, 0:SPAN], ALU.add).then_inc(eadded, 1)
                        dve.wait_ge(eadded, t * SC + k + 1)

                    if not last_layer:
                        dve.wait_ge(zeroed, 2)

                    def steps(t, n, ins):
                        ins.then_inc(step, 1)
                        dve.wait_ge(step, (t - 1) * 5 + n)

                    def body(t):
                        if has_node(t):
                            node_dve_scale(dve, nd, 1, t - 1)
                        if has_node(t) and last_layer:
                            nc.vector.tensor_tensor(agg[:, :], SE[:, bass.ds((t - 1) * BLOCK, BLOCK)], rcb[:, :], ALU.mult).then_inc(aggd, 1)
                            wide = (LO, SUBS, D)
                            dve.wait_ge(nd.mixed, t)
                            dve.wait_ge(x_ok, t * 16)
                            nc.vector.tensor_tensor(x1[:, :, :], ps_mix[0:LO, 0:SUBS * D].rearrange("p (k d) -> p k d", d=D),
                                                    x_in[:, :, :], ALU.add).then_inc(x1_ok, 1)
                            dve.wait_ge(x1_ok, t)
                            steps(t, 1, nc.vector.tensor_reduce(st[:, 0, :], x1[:, :, :], AX.X, ALU.add))
                            steps(t, 2, nc.vector.tensor_scalar(st[:, 0, :], st[:, 0, :], 1.0 / D, None, ALU.mult))
                            nc.vector.tensor_tensor(xc[:, :, :], x1[:, :, :], st[:, 0, :].unsqueeze(2).broadcast_to(wide),
                                                    ALU.subtract).then_inc(centred, 1)
                            dve.wait_ge(squared, t)
                            steps(t, 3, nc.vector.tensor_reduce(st[:, 1, :], sq[:, :, :], AX.X, ALU.add))
                            nc.vector.tensor_scalar(st[:, 1, :], st[:, 1, :], 1.0 / D, EPS, ALU.mult, ALU.add).then_inc(varied, 1)
                            dve.wait_ge(rooted, t)
                            steps(t, 4, nc.vector.reciprocal(st[:, 2, :], st[:, 1, :]))
                            nc.vector.tensor_tensor(xc[:, :, :], xc[:, :, :], st[:, 2, :].unsqueeze(2).broadcast_to(wide),
                                                    ALU.mult).then_inc(normed, 1)
                        if multiplies(t) and not last_layer:
                            if not has_node(t):
                                hots(t, 0)
                            hots(t, 1)
                            add(t, 0)
                            hots(t, 2)
                            if has_node(t):
                                node_dve_low(dve, nd, t - 1)
                            node_dve_scale(dve, nd, 0, t)
                            add(t, 1)
                            hots(t, 3)
                            add(t, 2)
                            if not is_last(t):
                                hots(t + 1, 0)
                            add(t, 3)
                        elif not last_layer:
                            node_dve_low(dve, nd, t - 1)
                        if multiplies(t) and last_layer:
                            node_dve_scale(dve, nd, 0, t)
                        if has_node(t) and last_layer:
                            dve.wait_ge(x1b_ok, t)
                            dve.wait_ge(p2, t)
                            dve.wait_ge(out_free, t)
                            nc.vector.tensor_tensor(result[:, :, :], ps_build[1][0:LO, 0, 0:SUBS * D].rearrange("p (k d) -> p k d", d=D),
                                                    x1b[:, :, :], ALU.add).then_inc(out_ok, 1)
                            steps(t, 5, nc.vector.tensor_copy(st[:, 2, 0:1], st[:, 2, 1:2]))
                    turns(dve, body)
                    if not last_layer:
                        dve.wait_ge(emaxed, NS)
                        nc.vector.tensor_reduce(top[:, 1:2], emax[:, :], AX.X, ALU.max).then_inc(emaxed, 1)
                        dve.wait_ge(emaxed, NS + 1)
                        nc.vector.tensor_tensor(flags[0:LO, 3:4], flags[0:LO, 3:4], top[:, 1:2], ALU.max).then_inc(emaxed, 1)

        for l in range(1, LAYERS):
            layer(l)

        with ExitStack() as part:
            ones_c = sb("ones_c", [P, 1], F32, part)
            tests = sb("tests", [P, 4], F32, part)
            sums = sb("sums", [1, 4], F32, part)
            set_, tested, added, step = sem("v_set", part), sem("v_tested", part), sem("v_added", part), sem("v_step", part)
            block = part.enter_context(nc.Block())

            @block.gpsimd
            def _(pool):
                nc.gpsimd.memset(ones_c[:, :], 1.0).then_inc(set_, 1)

            @block.tensor
            def _(pe):
                pe.wait_ge(set_, 1)
                pe.wait_ge(tested, 1)
                nc.tensor.matmul(ps_mix[0:1, 0:4], ones_c[:, :], tests[:, :], start=True, stop=True).then_inc(added, 1)

            @block.vector
            def _(dve):
                nc.vector.tensor_copy(tests[:, 0:2], flags[:, 0:2]).then_inc(step, 1)
                nc.vector.tensor_scalar(tests[:, 2:3], flags[:, 2:3], COUNT_BITS, None, ALU.is_gt).then_inc(step, 1)
                nc.vector.tensor_scalar(tests[:, 3:4], flags[:, 3:4], MAX_H, None, ALU.is_gt).then_inc(tested, 1)
                dve.wait_ge(added, 1)
                nc.vector.tensor_scalar(sums[:, 0:2], ps_mix[0:1, 0:2], float(E), None, ALU.not_equal).then_inc(step, 1)
                nc.vector.tensor_scalar(sums[:, 2:4], ps_mix[0:1, 2:4], 0.5, None, ALU.is_gt).then_inc(step, 1)
                dve.wait_ge(step, 4)
                nc.vector.tensor_reduce(verdict[0:1, 0:1], sums[:, :], AX.X, ALU.max).then_inc(step, 1)
                dve.wait_ge(step, 5)


def general_path(nc, x, src, dst, attr, Wl, Wr, b, W0, b0, W1, b1, W2, b2, out):
    with ExitStack() as ctx:
        def sb(name, shape, dt=F32):
            return ctx.enter_context(nc.sbuf_tensor("g_" + name, shape, dt))

        def pb(name, shape, dt=F32):
            return ctx.enter_context(nc.psum_tensor("g_" + name, shape, dt))

        def sem(name):
            return ctx.enter_context(nc.semaphore("g_" + name))

        table = nc.dram_tensor("g_table", (N, D), F32).ap()
        sums = [nc.dram_tensor(f"g_sums{i}", (N + GP, D + 1), F32).ap() for i in range(LAYERS + 1)]
        by_part = "(p t) d -> p t d"

        X = sb("X", [GP, GT, D])
        H = sb("H", [GP, GT, D])
        S = sb("S", [GP, GT, D + 1])
        rcnt = sb("rcnt", [GP, GT])
        stat = sb("stat", [GP, 2, GT])
        src_i = sb("src_i", [GP, GE], I32)
        dst_i = sb("dst_i", [GP, GE], I32)
        ident = sb("ident", [GP, GP])
        earlier = sb("earlier", [GP, GP])
        eq = sb("eq", [GP, GP])
        eqe = sb("eqe", [GP, GP])
        dcol = sb("dcol", [GP, 1])
        dup = sb("dup", [GP, 1])
        spare = sb("spare", [GP, 1])
        at_src = sb("at_src", [GP, 1], I32)
        at_dst = sb("at_dst", [GP, 1], I32)
        msg = sb("msg", [GP, D + 1])
        comb = sb("comb", [GP, D + 1])
        cat = sb("cat", [GP, 2 * D])
        catT = sb("catT", [2 * D, GP])
        y0 = sb("y0", [D, GP])
        y1 = sb("y1", [D, GP])
        w = sb("w", [2 * D, LAYERS, D])
        w0 = sb("w0", [2 * D, D])
        w1 = sb("w1", [D, D])
        w2 = sb("w2", [D, D])
        bias = sb("bias", [GP, LAYERS + 1, D])
        bias01 = sb("bias01", [D, 2])
        ps_dst = pb("ps_dst", [GP, GP])
        ps_comb = pb("ps_comb", [GP, D + 1])
        ps_T = pb("ps_T", [2 * D, GP])
        ps_a = pb("ps_a", [GP, D])
        ps_y0 = pb("ps_y0", [D, GP])
        ps_y1 = pb("ps_y1", [D, GP])

        loaded = sem("loaded")
        constants = sem("constants")
        const_step = sem("const_step")

        def layernorm_relu(steps, of, to):
            m, v = stat[:, 0, :], stat[:, 1, :]
            wide = (GP, GT, D)
            steps(nc.vector.tensor_reduce(m, of, AX.X, ALU.add))
            steps(nc.vector.tensor_scalar(m, m, 1.0 / D, None, ALU.mult))
            steps(nc.vector.tensor_tensor(to, of, m.unsqueeze(2).broadcast_to(wide), ALU.subtract))
            steps(nc.vector.tensor_tensor(S[:, :, 0:D], to, to, ALU.mult))
            steps(nc.vector.tensor_reduce(v, S[:, :, 0:D], AX.X, ALU.add))
            steps(nc.vector.tensor_scalar(v, v, 1.0 / D, EPS, ALU.mult, ALU.add))

        with ExitStack() as part:
            varied = part.enter_context(nc.semaphore("g_varied"))
            rooted = part.enter_context(nc.semaphore("g_rooted"))
            dve_step = part.enter_context(nc.semaphore("g_dve_step0"))
            zeroed = part.enter_context(nc.semaphore("g_zeroed"))
            normed = part.enter_context(nc.semaphore("g_normed"))
            stored = part.enter_context(nc.semaphore("g_stored0"))
            block = part.enter_context(nc.Block())

            @block.sync
            def _(sp):
                sp.dma_start(X[:, :, :], x.rearrange(by_part, p=GP)).then_inc(loaded, 16)
                sp.dma_start(src_i[:, :], src.rearrange("(p j) -> p j", p=GP)).then_inc(loaded, 16)
                sp.dma_start(dst_i[:, :], dst.rearrange("(p j) -> p j", p=GP)).then_inc(loaded, 16)
                sp.dma_start(w[0:D, :, :], Wl.rearrange("l i o -> i l o")).then_inc(loaded, 16)
                sp.dma_start(w[D:2 * D, :, :], Wr.rearrange("l i o -> i l o")).then_inc(loaded, 16)
                sp.dma_start(w0[:, :], W0).then_inc(loaded, 16)
                sp.dma_start(w1[:, :], W1).then_inc(loaded, 16)
                sp.dma_start(w2[:, :], W2).then_inc(loaded, 16)
                for i in range(LAYERS):
                    sp.dma_start(bias[:, i, :], b[i:i + 1, :].broadcast_to((GP, D))).then_inc(loaded, 16)
                sp.dma_start(bias[:, LAYERS, :], b2.unsqueeze(0).broadcast_to((GP, D))).then_inc(loaded, 16)
                sp.dma_start(bias01[:, 0:1], b0.unsqueeze(1)).then_inc(loaded, 16)
                sp.dma_start(bias01[:, 1:2], b1.unsqueeze(1)).then_inc(loaded, 16)
                sp.wait_ge(zeroed, 1)
                for i in range(LAYERS + 1):
                    sp.dma_start(sums[i][0:N, :].rearrange(by_part, p=GP), S[:, :, :]).then_inc(stored, 16)
                    sp.dma_start(sums[i][N:N + GP, :], S[:, 0, :]).then_inc(stored, 16)
                sp.wait_ge(normed, 1)
                sp.dma_start(table.rearrange(by_part, p=GP), H[:, :, :]).then_inc(stored, 16)
                sp.wait_ge(stored, 16 * (2 * LAYERS + 3))
                sp.wait_ge(loaded, 16 * 14)

            @block.gpsimd
            def _(pool):
                nc.gpsimd.memset(ident[:, :], 0.0).then_inc(const_step, 1)
                nc.gpsimd.memset(earlier[:, :], 1.0).then_inc(const_step, 1)
                pool.wait_ge(const_step, 2)
                nc.gpsimd.affine_select(out=ident[:, :], in_=ident[:, :], compare_op=ALU.not_equal, fill=1.0,
                                        base=0, pattern=[[-1, GP]], channel_multiplier=1).then_inc(constants, 1)
                nc.gpsimd.affine_select(out=earlier[:, :], in_=earlier[:, :], compare_op=ALU.is_gt, fill=0.0,
                                        base=0, pattern=[[-1, GP]], channel_multiplier=1).then_inc(constants, 1)
                nc.gpsimd.memset(msg[:, :], 1.0).then_inc(constants, 1)
                nc.gpsimd.iota(spare[:, :], pattern=[[0, 1]], base=N, channel_multiplier=1,
                               allow_small_or_imprecise_dtypes=True).then_inc(constants, 1)

            @block.scalar
            def _(act):
                act.wait_ge(varied, 1)
                nc.scalar.activation(stat[:, 1, :], stat[:, 1, :], ACT.Sqrt).then_inc(rooted, 1)

            @block.tensor
            def _(pe):
                pe.wait_ge(constants, 4)

            @block.vector
            def _(dve):
                count = [0]

                def steps(ins):
                    count[0] += 1
                    ins.then_inc(dve_step, 1)
                    dve.wait_ge(dve_step, count[0])

                nc.vector.memset(S[:, :, :], 0.0).then_inc(zeroed, 1)
                dve.wait_ge(loaded, 16 * 14)
                dve.wait_ge(stored, 16 * (2 * LAYERS + 2))
                layernorm_relu(steps, X[:, :, :], H[:, :, :])
                nc.vector.tensor_copy(stat[:, 0, :], stat[:, 0, :]).then_inc(varied, 1)
                dve.wait_ge(rooted, 1)
                steps(nc.vector.reciprocal(stat[:, 1, :], stat[:, 1, :]))
                steps(nc.vector.tensor_tensor(H[:, :, :], H[:, :, :],
                                              stat[:, 1, :].unsqueeze(2).broadcast_to((GP, GT, D)), ALU.mult))
                nc.vector.tensor_scalar(H[:, :, :], H[:, :, :], 0.0, None, ALU.max).then_inc(normed, 1)

        def edge_block(i):
            with ExitStack() as part:
                def s(name):
                    return part.enter_context(nc.semaphore(f"g_{name}{i}"))

                turns, indexed, transposed, equal, summed, ready = s("turns"), s("indexed"), s("transposed"), s("equal"), s("summed"), s("ready")
                gathered, scattered, dve_step = s("gathered"), s("scattered"), s("dve_step")
                block = part.enter_context(nc.Block())

                @block.gpsimd
                def _(pool):
                    with pool.Fori(0, GE) as j:
                        pool.wait_ge(indexed, j + 1)
                        pool.sem_inc(turns, 1)
                        if i < LAYERS:
                            nc.gpsimd.indirect_dma_start(
                                out=msg[:, 0:D], out_offset=None, in_=table[:, :],
                                in_offset=bass.IndirectOffsetOnAxis(ap=at_src[:, 0:1], axis=0)).then_inc(gathered, 16)
                        else:
                            pool.dma_start(msg[:, 0:D],
                                           attr.rearrange("(p j) d -> p j d", p=GP)[:, bass.ds(j, 1), :]
                                           .rearrange("p j d -> p (j d)")).then_inc(gathered, 16)
                        pool.wait_ge(ready, j + 1)
                        pool.sem_inc(turns, 1)
                        nc.gpsimd.indirect_dma_start(
                            out=sums[i][:, :], out_offset=bass.IndirectOffsetOnAxis(ap=at_dst[:, 0:1], axis=0),
                            in_=comb[:, :], in_offset=None,
                            compute_op=ALU.add).then_inc(scattered, 16)
                        pool.wait_ge(scattered, 16 * j + 16)

                @block.tensor
                def _(pe):
                    with pe.Fori(0, GE) as j:
                        pe.wait_ge(indexed, j + 1)
                        nc.tensor.transpose(ps_dst[:, :], dcol[:, 0:1].broadcast_to((GP, GP)), ident[:, :]).then_inc(transposed, 1)
                        pe.wait_ge(equal, j + 1)
                        pe.wait_ge(gathered, 16 * j + 16)
                        nc.tensor.matmul(ps_comb[:, :], eq[:, :], msg[:, :], start=True, stop=True).then_inc(summed, 1)

                @block.vector
                def _(dve):
                    with dve.Fori(0, GE) as j:
                        def step(ins, k):
                            ins.then_inc(dve_step, 1)
                            dve.wait_ge(dve_step, 6 * j + k)

                        step(nc.vector.tensor_copy(at_src[:, :], src_i[:, bass.ds(j, 1)]), 1)
                        nc.vector.tensor_copy(dcol[:, :], dst_i[:, bass.ds(j, 1)]).then_inc(indexed, 1)
                        dve.wait_ge(transposed, j + 1)
                        step(nc.vector.tensor_scalar(eq[:, :], ps_dst[:, :], dcol[:, 0:1], None, ALU.is_equal), 2)
                        step(nc.vector.tensor_tensor(eqe[:, :], eq[:, :], earlier[:, :], ALU.mult), 3)
                        step(nc.vector.tensor_reduce(dup[:, :], eqe[:, :], AX.X, ALU.max), 4)
                        step(nc.vector.tensor_scalar(dup[:, :], spare[:, :], dcol[:, 0:1], dup[:, 0:1],
                                                     ALU.subtract, ALU.mult), 5)
                        nc.vector.tensor_tensor(at_dst[:, :], dup[:, :], dcol[:, :], ALU.add).then_inc(equal, 1)
                        dve.wait_ge(summed, j + 1)
                        step(nc.vector.tensor_copy(comb[:, :], ps_comb[:, :]), 6)
                        nc.vector.tensor_copy(dup[:, :], dup[:, :]).then_inc(ready, 1)
                        dve.wait_ge(scattered, 16 * j + 16)

        def node_block(i):
            last = i == LAYERS
            with ExitStack() as part:
                def s(name):
                    return part.enter_context(nc.semaphore(f"g_{name}n{i}"))

                landed, joined, turned, turned_sb, mixed = s("landed"), s("joined"), s("turned"), s("turned_sb"), s("mixed")
                y0_ps, y0_sb, y1_ps, y1_sb, done, stored, dve_step = (
                    s("y0_ps"), s("y0_sb"), s("y1_ps"), s("y1_sb"), s("done"), s("stored"), s("dve_step"))
                varied, rooted = s("varied"), s("rooted")
                block = part.enter_context(nc.Block())
                to_dram = out if last else table

                @block.sync
                def _(sp):
                    sp.dma_start(S[:, :, :], sums[i][0:N, :].rearrange(by_part, p=GP)).then_inc(landed, 16)
                    if i == LAYERS - 1:
                        return
                    sp.wait_ge(done, 1)
                    sp.dma_start(to_dram.rearrange(by_part, p=GP), (X if last else H)[:, :, :]).then_inc(stored, 16)
                    sp.wait_ge(stored, 16)

                @block.tensor
                def _(pe):
                    with pe.Fori(0, GT) as t:
                        pe.wait_ge(joined, t + 1)
                        nc.tensor.transpose(ps_T[:, :], cat[:, :], ident[:, :]).then_inc(turned, 1)
                        pe.wait_ge(turned_sb, t + 1)
                        if not last:
                            nc.tensor.matmul(ps_a[:, :], catT[:, :], w[:, i, :], start=True, stop=True).then_inc(mixed, 1)
                        else:
                            nc.tensor.matmul(ps_y0[:, :], w0[:, :], catT[:, :], start=True, stop=True).then_inc(y0_ps, 1)
                            pe.wait_ge(constants, 4)
                            pe.wait_ge(y0_sb, t + 1)
                            nc.tensor.matmul(ps_y1[:, :], w1[:, :], y0[:, :], start=True, stop=True).then_inc(y1_ps, 1)
                            pe.wait_ge(constants, 4)
                            pe.wait_ge(y1_sb, t + 1)
                            nc.tensor.matmul(ps_a[:, :], y1[:, :], w2[:, :], start=True, stop=True).then_inc(mixed, 1)

                @block.scalar
                def _(act):
                    if last:
                        with act.Fori(0, GT) as t:
                            act.wait_ge(y0_ps, t + 1)
                            nc.scalar.activation(y0[:, :], ps_y0[:, :], ACT.Relu, bias=bias01[:, 0:1]).then_inc(y0_sb, 1)
                            act.wait_ge(y1_ps, t + 1)
                            nc.scalar.activation(y1[:, :], ps_y1[:, :], ACT.Relu, bias=bias01[:, 1:2]).then_inc(y1_sb, 1)
                    if i == LAYERS - 1:
                        act.wait_ge(varied, 1)
                        nc.scalar.activation(stat[:, 1, :], stat[:, 1, :], ACT.Sqrt).then_inc(rooted, 1)

                @block.vector
                def _(dve):
                    dve.wait_ge(landed, 16)
                    nc.vector.tensor_scalar(rcnt[:, :], S[:, :, D], 1.0, None, ALU.max).then_inc(dve_step, 1)
                    dve.wait_ge(dve_step, 1)
                    nc.vector.reciprocal(rcnt[:, :], rcnt[:, :]).then_inc(dve_step, 1)
                    dve.wait_ge(dve_step, 2)
                    with dve.Fori(0, GT) as t:
                        def step(ins, k):
                            ins.then_inc(dve_step, 1)
                            dve.wait_ge(dve_step, 3 * t + 2 + k)

                        def row(a):
                            return a[:, bass.ds(t, 1), 0:D].rearrange("p t d -> p (t d)")

                        step(nc.vector.tensor_scalar(cat[:, 0:D], row(S), rcnt[:, bass.ds(t, 1)], None, ALU.mult), 1)
                        nc.vector.tensor_copy(cat[:, D:2 * D], row(H)).then_inc(joined, 1)
                        dve.wait_ge(turned, t + 1)
                        nc.vector.tensor_copy(catT[:, :], ps_T[:, :]).then_inc(turned_sb, 1)
                        dve.wait_ge(mixed, t + 1)
                        if i < LAYERS - 1:
                            step(nc.vector.tensor_tensor(row(H), ps_a[:, :], bias[:, i, :], ALU.add), 2)
                            step(nc.vector.tensor_scalar(row(H), row(H), 0.0, None, ALU.max), 3)
                        else:
                            step(nc.vector.tensor_tensor(row(H), ps_a[:, :], bias[:, i, :], ALU.add), 2)
                            step(nc.vector.tensor_tensor(row(X), row(H), row(X), ALU.add), 3)
                    count = [3 * GT + 2]

                    def steps(ins):
                        count[0] += 1
                        ins.then_inc(dve_step, 1)
                        dve.wait_ge(dve_step, count[0])

                    if i == LAYERS - 1:
                        layernorm_relu(steps, X[:, :, :], H[:, :, :])
                        nc.vector.tensor_copy(stat[:, 0, :], stat[:, 0, :]).then_inc(varied, 1)
                        dve.wait_ge(rooted, 1)
                        steps(nc.vector.reciprocal(stat[:, 1, :], stat[:, 1, :]))
                        steps(nc.vector.tensor_tensor(H[:, :, :], H[:, :, :],
                                                      stat[:, 1, :].unsqueeze(2).broadcast_to((GP, GT, D)), ALU.mult))
                        steps(nc.vector.tensor_scalar(H[:, :, :], H[:, :, :], 0.0, None, ALU.max))
                    nc.vector.tensor_copy(rcnt[:, :], rcnt[:, :]).then_inc(done, 1)

        for i in range(LAYERS + 1):
            edge_block(i)
            node_block(i)


def both_paths(nc, *args):
    with ExitStack() as ctx:
        verdict = ctx.enter_context(nc.sbuf_tensor("verdict", [1, 1], I32))
        cleared = ctx.enter_context(nc.semaphore("cleared"))
        used = []
        dense_path(nc, *args, verdict, used, ctx)
        refused = nc.values_load(verdict[0:1, 0:1], min_val=0, max_val=1)
        with nc.If(refused > 0):
            with nc.Block() as block:
                @block.gpsimd
                def _(pool):
                    for s in used:
                        pool.sem_clear(s)
                    pool.sem_inc(cleared, 1)

                @block.sync
                def _(sp):
                    sp.wait_ge(cleared, 1)

                @block.tensor
                def _(pe):
                    pe.wait_ge(cleared, 1)

                @block.scalar
                def _(act):
                    act.wait_ge(cleared, 1)

                @block.vector
                def _(dve):
                    dve.wait_ge(cleared, 1)

            general_path(nc, *args)


_INS = ['x', 'src', 'dst', 'edge_attr_64', 'L0_gnn_Wl', 'L0_gnn_Wr', 'L0_gnn_b', 'L1_gnn_W0', 'L1_gnn_b0',
        'L1_gnn_W1', 'L1_gnn_b1', 'L1_gnn_W2', 'L1_gnn_b2']


def kernel(**inputs):
    import numpy as _np
    import concourse.bacc as _bacc
    from concourse import mybir as _mybir
    from concourse.bass_utils import run_bass_kernel_spmd as _run

    nc = _bacc.Bacc("TRN2", target_bir_lowering=False, num_devices=1)
    arrays, args = {}, []
    for name in _INS:
        a = _np.ascontiguousarray(inputs[name])
        arrays[f"in_{name}"] = a
        args.append(nc.dram_tensor(f"in_{name}", a.shape, _mybir.dt.from_np(a.dtype), kind="ExternalInput").ap())
    out = nc.dram_tensor("out_0", (N, D), _mybir.dt.float32, kind="ExternalOutput").ap()
    both_paths(nc, *args, out)
    r = _run(nc, [arrays], core_ids=[0])
    return r.results[0]["out_0"]
```
